# Optimizing a Trainium2 kernel written in Bass

```python
import numpy as np
import jax
import jax.numpy as jnp

def _softmax(x, axis=-1):
    return jax.nn.softmax(x, axis=axis)

def _gelu(x):
    return jax.nn.gelu(x, approximate=True)

def _silu(x):
    return jax.nn.silu(x)

def _sigmoid(x):
    return jax.nn.sigmoid(x)

def _layernorm(x, axis=-1, eps=1e-05):
    m = jnp.mean(x, axis=axis, keepdims=True)
    v = jnp.var(x, axis=axis, keepdims=True)
    return (x - m) / jnp.sqrt(v + eps)

def _scatter_add(tgt, idx, src, axis=0):
    return tgt.at[idx].add(src)

def _segment_sum(src, seg, n):
    return jax.ops.segment_sum(src, seg, n)
kernel_name = 'mk_adaln_d1_jaxref_r8_a8bb87'

def setup_inputs(seed: int=0):
    np.random.seed(seed)
    _w = jnp.asarray

    def _L0_attn_setup():
        import jax, jax.numpy as jnp
        from jax import lax
        import numpy as np
        import math
        B, L, D_MODEL = (2, 512, 128)
        D_INNER = 2 * D_MODEL
        D_STATE = 16
        D_CONV = 4
        DT_RANK = math.ceil(D_MODEL / 16)

        def _xavier(key, shape):
            fan_out, fan_in = (shape[0], shape[1])
            a = (6.0 / (fan_in + fan_out)) ** 0.5
            return jax.random.uniform(key, shape, jnp.float32, -a, a)
        key = jax.random.key(seed)
        ks = jax.random.split(key, 8)
        conv_w = jnp.zeros((D_INNER, 1, D_CONV), jnp.float32).at[:, 0, -1].set(1.0)
        dt_init = jnp.full((D_INNER,), 0.1, jnp.float32)
        dt_b = dt_init + jnp.log(-jnp.expm1(-dt_init))
        a_init = jnp.tile(jnp.arange(1, D_STATE + 1, dtype=jnp.float32), (D_INNER, 1))
        return {'hidden_states': jax.random.normal(ks[0], (B, L, D_MODEL), jnp.float32), 'in_proj_w': _xavier(ks[1], (2 * D_INNER, D_MODEL)), 'conv_w': conv_w, 'conv_b': jnp.zeros((D_INNER,), jnp.float32), 'x_proj_w': _xavier(ks[2], (DT_RANK + 2 * D_STATE, D_INNER)), 'dt_w': _xavier(ks[3], (D_INNER, DT_RANK)), 'dt_b': dt_b, 'A_log': jnp.log(a_init), 'D': jnp.ones((D_INNER,), jnp.float32), 'out_proj_w': _xavier(ks[4], (D_MODEL, D_INNER))}
    _L0_attn_in = _L0_attn_setup()

    def _L0_ffn_setup():
        import jax, jax.numpy as jnp
        import numpy as np
        D = 128
        H = 256
        E = 8
        TOP_K = 2
        N_SHARED = 1
        B, S = (2, 128)
        key = jax.random.key(seed)
        ks = jax.random.split(key, 12)
        sc = 0.02
        return {'hidden': jax.random.normal(ks[0], (B, S, D), jnp.float32), 'router_w': jax.random.normal(ks[1], (D, E), jnp.float32) * sc, 'router_b': jnp.zeros((E,), jnp.float32), 'sw1': jax.random.normal(ks[2], (D, H), jnp.float32) * sc, 'sb1': jnp.zeros((H,), jnp.float32), 'sw2': jax.random.normal(ks[3], (H, D), jnp.float32) * sc, 'sb2': jnp.zeros((D,), jnp.float32), 'rw1': jax.random.normal(ks[4], (E, D, H), jnp.float32) * sc, 'rb1': jnp.zeros((E, H), jnp.float32), 'rw2': jax.random.normal(ks[5], (E, H, D), jnp.float32) * sc, 'rb2': jnp.zeros((E, D), jnp.float32)}
    _L0_ffn_in = _L0_ffn_setup()
    _L0_c = _w((lambda *s: np.random.randn(*s).astype(np.float32) * 0.05)(8, 128))
    _L0_wmod = _w((lambda *s: np.random.randn(*s).astype(np.float32) * 0.05)(128, 6 * 128) * 128 ** (-0.5))
    _d = {'L0_attn_hidden_states': _L0_attn_in['hidden_states'], 'L0_attn_in_proj_w': _L0_attn_in['in_proj_w'], 'L0_attn_conv_w': _L0_attn_in['conv_w'], 'L0_attn_conv_b': _L0_attn_in['conv_b'], 'L0_attn_x_proj_w': _L0_attn_in['x_proj_w'], 'L0_attn_dt_w': _L0_attn_in['dt_w'], 'L0_attn_dt_b': _L0_attn_in['dt_b'], 'L0_attn_A_log': _L0_attn_in['A_log'], 'L0_attn_D': _L0_attn_in['D'], 'L0_attn_out_proj_w': _L0_attn_in['out_proj_w'], 'L0_ffn_router_w': _L0_ffn_in['router_w'], 'L0_ffn_router_b': _L0_ffn_in['router_b'], 'L0_ffn_sw1': _L0_ffn_in['sw1'], 'L0_ffn_sb1': _L0_ffn_in['sb1'], 'L0_ffn_sw2': _L0_ffn_in['sw2'], 'L0_ffn_sb2': _L0_ffn_in['sb2'], 'L0_ffn_rw1': _L0_ffn_in['rw1'], 'L0_ffn_rb1': _L0_ffn_in['rb1'], 'L0_ffn_rw2': _L0_ffn_in['rw2'], 'L0_ffn_rb2': _L0_ffn_in['rb2'], 'L0_c': _L0_c, 'L0_wmod': _L0_wmod}
    _x0 = _d['L0_attn_hidden_states']
    _d['L0_attn_hidden_states'] = jax.random.normal(jax.random.fold_in(jax.random.key(seed), 1), (8, 512, 128), dtype=_x0.dtype)
    del _x0
    return _d

def reference(L0_attn_hidden_states, L0_attn_in_proj_w, L0_attn_conv_w, L0_attn_conv_b, L0_attn_x_proj_w, L0_attn_dt_w, L0_attn_dt_b, L0_attn_A_log, L0_attn_D, L0_attn_out_proj_w, L0_ffn_router_w, L0_ffn_router_b, L0_ffn_sw1, L0_ffn_sb1, L0_ffn_sw2, L0_ffn_sb2, L0_ffn_rw1, L0_ffn_rb1, L0_ffn_rw2, L0_ffn_rb2, L0_c, L0_wmod):

    def _L0_attn_ref(hidden_states, in_proj_w, conv_w, conv_b, x_proj_w, dt_w, dt_b, A_log, D, out_proj_w):
        import jax, jax.numpy as jnp
        from jax import lax
        import numpy as np
        import math
        B, L, D_MODEL = (2, 512, 128)
        D_INNER = 2 * D_MODEL
        D_STATE = 16
        D_CONV = 4
        DT_RANK = math.ceil(D_MODEL / 16)

        def _xavier(key, shape):
            fan_out, fan_in = (shape[0], shape[1])
            a = (6.0 / (fan_in + fan_out)) ** 0.5
            return jax.random.uniform(key, shape, jnp.float32, -a, a)
        b, l, _ = hidden_states.shape
        d_inner = conv_w.shape[0]
        n = A_log.shape[1]
        dt_rank = dt_w.shape[1]
        d_conv = conv_w.shape[-1]
        xz = hidden_states @ in_proj_w.T
        x, z = jnp.split(xz, 2, axis=-1)
        x_t = x.transpose(0, 2, 1)
        x_conv = lax.conv_general_dilated(x_t, conv_w, window_strides=(1,), padding=[(d_conv - 1, 0)], dimension_numbers=('NCH', 'OIH', 'NCH'), feature_group_count=d_inner) + conv_b[None, :, None]
        x_bld = jax.nn.silu(x_conv).transpose(0, 2, 1)
        xp = x_bld @ x_proj_w.T
        dt, Bm, Cm = jnp.split(xp, [dt_rank, dt_rank + n], axis=-1)
        delta = jax.nn.softplus(dt @ dt_w.T + dt_b)
        A = -jnp.exp(A_log)

        def step(h, inp):
            d_t, u_t, b_t, c_t = inp
            dA = jnp.exp(d_t[..., None] * A)
            h = h * dA + (d_t * u_t)[..., None] * b_t[:, None, :]
            y_t = jnp.einsum('bdn,bn->bd', h, c_t)
            return (h, y_t)
        h0 = jnp.zeros((b, d_inner, n), hidden_states.dtype)
        xs = (delta.transpose(1, 0, 2), x_bld.transpose(1, 0, 2), Bm.transpose(1, 0, 2), Cm.transpose(1, 0, 2))
        _, ys = lax.scan(step, h0, xs)
        y = ys.transpose(1, 0, 2) + x_bld * D
        y = y * jax.nn.silu(z)
        return y @ out_proj_w.T

    def _L0_ffn_ref(hidden, router_w, router_b, sw1, sb1, sw2, sb2, rw1, rb1, rw2, rb2):
        import jax, jax.numpy as jnp
        import numpy as np
        D = 128
        H = 256
        E = 8
        TOP_K = 2
        N_SHARED = 1
        B, S = (2, 128)
        b, s, d = hidden.shape
        T = b * s
        flat = hidden.reshape(T, d)
        router_logits = flat @ router_w + router_b
        router_probs = jax.nn.softmax(router_logits, axis=-1)
        topk_probs, topk_idx = jax.lax.top_k(router_probs, TOP_K)
        weights = jnp.zeros_like(router_probs).at[jnp.arange(T)[:, None], topk_idx].add(topk_probs)
        sh = jax.nn.gelu(flat @ sw1 + sb1, approximate=False)
        shared_out = (sh @ sw2 + sb2) / N_SHARED
        h1 = jax.nn.gelu(jnp.einsum('td,edh->teh', flat, rw1) + rb1[None], approximate=False)
        expert_out = jnp.einsum('teh,ehd->ted', h1, rw2) + rb2[None]
        mixed = jnp.einsum('ted,te->td', expert_out, weights)
        return (shared_out + mixed).reshape(b, s, d)
    x = L0_attn_hidden_states
    mod = (_silu(L0_c) @ L0_wmod).reshape(L0_c.shape[0], 6, 1, -1)
    sa, ca, ga, sb, cb, gb = (mod[:, 0], mod[:, 1], mod[:, 2], mod[:, 3], mod[:, 4], mod[:, 5])
    ga = (2 * (ga >= 0) - 1) * jnp.maximum(jnp.abs(ga), 0.25)
    gb = (2 * (gb >= 0) - 1) * jnp.maximum(jnp.abs(gb), 0.25)
    h = _layernorm(x, axis=-1) * (1 + ca) + sa
    x = x + ga * _L0_attn_ref(h, L0_attn_in_proj_w, L0_attn_conv_w, L0_attn_conv_b, L0_attn_x_proj_w, L0_attn_dt_w, L0_attn_dt_b, L0_attn_A_log, L0_attn_D, L0_attn_out_proj_w)
    h = _layernorm(x, axis=-1) * (1 + cb) + sb
    x = x + gb * _L0_ffn_ref(h, L0_ffn_router_w, L0_ffn_router_b, L0_ffn_sw1, L0_ffn_sb1, L0_ffn_sw2, L0_ffn_sb2, L0_ffn_rw1, L0_ffn_rb1, L0_ffn_rw2, L0_ffn_rb2)
    return x

_drawn_inputs = setup_inputs


def setup_inputs(seed=0):
    import zlib

    import numpy as np

    out = dict(_drawn_inputs(seed))
    spreads = {'L0_attn_conv_b': (0.0, 0.8),
     'L0_attn_dt_b': (-2.252168655395508, 0.6),
     'L0_attn_D': (1.0, 0.6),
     'L0_ffn_router_b': (0.0, 2.0),
     'L0_ffn_sb1': (0.0, 2.0),
     'L0_ffn_sb2': (0.0, 2.0),
     'L0_ffn_rb1': (0.0, 2.0),
     'L0_ffn_rb2': (0.0, 2.0)}
    factors = {'L0_attn_x_proj_w': 8.0,
     'L0_attn_dt_w': 8.0,
     'L0_attn_A_log': 8.0,
     'L0_ffn_router_w': 64.0,
     'L0_ffn_sw1': 48.536,
     'L0_ffn_sw2': 44.24,
     'L0_ffn_rw1': 64.0,
     'L0_ffn_rw2': 64.0}
    for name, (base, spread) in spreads.items():
        noise = np.random.default_rng([zlib.crc32(name.encode()), seed]).standard_normal(out[name].shape)
        drawn = base * np.exp(spread * noise) if base else spread * noise
        out[name] = jnp.asarray(drawn.astype(out[name].dtype))
    for name, factor in factors.items():
        out[name] = (out[name] * factor).astype(out[name].dtype)
    return out
```

```python
from contextlib import ExitStack

import concourse.bass as bass
from concourse import mybir

F32 = mybir.dt.float32
ALU = mybir.AluOpType
ACT = mybir.ActivationFunctionType
AX = mybir.AxisListType

B, L, DM = 8, 512, 128
DI = 2 * DM
NS = 16
R = 8
KC = 4
E, H = 8, 256
P = 128
NT = L // P
Q = DI // P
HQ = H // P
NG = 4
NC = NS // NG
CH = NC * Q
M_UP = (E + 1) * HQ
EPS = 1e-5
GATE_MIN = 0.25
STATE_RING = 4
DECAY_RING = 4
BC_RING = 2
POOL_INPUT_CHUNKS = (1, 4, 6)
ROW_RB1, ROW_SB1, ROW_CONVB, ROW_DTB, ROW_D, ROWS = 0, 16, 18, 20, 22, 24
SA, CA, GA, SB, CB, GB = range(6)


class Batch:

    def __init__(self, index, parity):
        self.i = index
        self.p = parity


def adaln_mamba_moe_kernel(nc, x, in_proj_w, conv_w, conv_b, x_proj_w, dt_w, dt_b, a_log, d_skip,
                           out_proj_w, router_w, router_b, sw1, sb1, sw2, sb2, rw1, rb1, rw2, rb2,
                           cond, wmod, out):
    bc_dram = nc.dram_tensor("bc_rows", [B, 2 * NS, L], F32).ap()
    gate_dram = nc.dram_tensor("gate_rows", [B, 2 * DM], F32).ap()

    with ExitStack() as ctx:
        def sb(name, shape, dtype=F32):
            return ctx.enter_context(nc.sbuf_tensor(name, shape, dtype))

        def sem(name):
            return ctx.enter_context(nc.semaphore(name))

        ident = sb("ident", [P, P])
        conv_in_wT = sb("conv_in_wT", [P, Q, KC, P])
        z_wT = sb("z_wT", [P, DI])
        xp_wT = sb("xp_wT", [P, Q, 2 * NS + R])
        small_w = sb("small_w", [P, Q * P])
        out_wT = sb("out_wT", [P, Q, DM])
        router_sb = sb("router_sb", [P, E])
        router_bias = sb("router_bias", [P, E])
        up_w = sb("up_w", [P, E + 1, H])
        down_w = sb("down_w", [P, E + 1, HQ, DM])
        vec = sb("vec", [P, ROWS])
        a_neg = sb("a_neg", [P, Q, NS])
        modT = sb("modT", [P, 4, B])
        constants = sb("constants", [P, 2 * NT])
        minus_half, eps_tile = constants[:, 0:NT], constants[:, NT:2 * NT]
        before = sb("before", [P, E, E], mybir.dt.bfloat16)
        x_sb = sb("x_sb", [P, NT, DM])
        h_sb = sb("h_sb", [P, KC - 1 + L])
        du = sb("du", [P, 2, Q, L])
        skip = sb("skip", [P, Q, L])
        z_silu = sb("z_silu", [P, 2, NT, DI])
        rows = sb("rows", [P, L])
        delta = sb("delta", [P, 2, Q, L])
        decay = sb("decay", [P, DECAY_RING, NG, L])
        state = sb("state", [P, STATE_RING, NG, L])
        bc = sb("bc", [P, BC_RING, 2, NG, L])
        gT_mix = sb("gT_mix", [P, NT * DI])
        g_soft = sb("g_soft", [P, Q, L])
        x1 = sb("x1", [P, NT, DM])
        gates = sb("gates", [P, 2, DM])
        h2 = sb("h2", [P, L])
        h1 = sb("h1", [P, M_UP, L])
        w9 = sb("w9", [P, NT, E + 1])
        out_sb = sb("out_sb", [P, NT, DM])
        bn = sb("bn", [P, NT, 6])
        mean_var = sb("mean_var", [P, 2, NT, 2])
        rstd = sb("rstd", [P, 2, NT])
        router_stats = sb("router_stats", [P, 2 * NT + 1])
        rmax, rsum = router_stats[:, 0:NT], router_stats[:, NT:2 * NT]
        pace = router_stats[:, 2 * NT:2 * NT + 1]

        gT = gT_mix[:, :].rearrange("p (t c) -> p t c", t=NT)
        mix = gT_mix[:, :].rearrange("p (e d) -> p e d", e=E)
        gt_eq = gT_mix[:, 0:2 * NT * E * E].rearrange("p (g t e j) -> p g t e j", g=2, t=NT, e=E)
        lg, ex, pr, rank = (gT_mix[:, k * NT * E:(k + 1) * NT * E].rearrange("p (t e) -> p t e", t=NT)
                            for k in range(2 * E, 2 * E + 4))
        xhat2 = out_sb
        bcdt = rows[0:2 * NS + R, :]
        w9T = rows[64:64 + E + 1, :]
        dt_wT = small_w[0:2 * NS + R, :].rearrange("p (q d) -> p q d", q=Q)
        down_bias = small_w[64:64 + E + 1, 0:DM]
        raw = state[:, :, :, :].rearrange("p r n t -> p (r n t)")
        in_raw = raw[:, 0:4 * DM].rearrange("p (j d) -> p j d", j=4)
        conv_raw = raw[:, 512:512 + Q * KC].rearrange("p (q k) -> p q k", q=Q)
        conv_in_raw = raw[:, 1024:2048].rearrange("p (q k d) -> p q k d", q=Q, k=KC)
        xp_raw = raw[0:2 * NS + R, 2048:2048 + DI]
        dt_raw = raw[:, 2560:2560 + Q * (2 * NS + R)].rearrange("p (q r) -> p q r", q=Q)
        out_raw = raw[:, 3072:3072 + DI]
        vec_raw = raw[0:ROWS, 3584:3584 + P]
        cond_raw = raw[0:B, 3712:3712 + DM]
        condT = raw[:, 3840:3840 + B]
        a_raw = raw[:, 3904:3904 + Q * NS].rearrange("p (q n) -> p q n", q=Q)
        gate_raw = raw[0:B, 4096:4096 + 2 * DM]
        gate_sign = raw[0:B, 4352:4352 + 2 * DM]
        gate_abs = raw[0:B, 4608:4608 + 2 * DM]
        wmod_sb = raw[:, 5120:5120 + 6 * DM]

        psum = ctx.enter_context(nc.psum_tensor("psum", [P, 8, 512], F32))
        Y = (psum[:, 0, :], psum[:, 1, :])
        WORK = (psum[:, 2, :], psum[:, 3, :])
        WIDE = psum[:, 4:6, :].rearrange("p a c -> p (a c)")
        OUTP = psum[:, 6, :]
        MISC = psum[:, 7, :]

        w_in = sem("weights_in")
        x_in = sem("x_in")
        x1_in = sem("residual_and_gates_in")
        bc_stored = sem("bc_stored")
        bc_in = [sem(f"bc_in{i}") for i in range(BC_RING)]
        gates_stored = sem("gates_stored")
        out_stored = sem("out_stored")
        const_made = sem("const_made")
        raw_ready = sem("conv_scaled")
        set_mm = sem("setup_matmul")
        set_ev = sem("setup_evacuated")
        cond_silu = sem("cond_silu")
        gate_steps = sem("gate_steps")
        a_exp = sem("a_exp")
        setup_done = sem("setup_done")
        bn_done = sem("bn_done")
        stats_done = sem("stats_done")
        rstd_done = sem("rstd_done")
        rstd_eps = sem("rstd_eps")
        xhat_done = sem("xhat_done")
        xT_done = sem("xT_done")
        h_done = sem("h_done")
        conv_done = sem("conv_done")
        xb_done = sem("xb_done")
        z_done = sem("z_done")
        zs_done = sem("zs_done")
        xproj_done = sem("xproj_done")
        bcdt_done = sem("bcdt_done")
        dt_done = sem("dt_done")
        sp_abs = sem("softplus_abs")
        sp_relu = sem("softplus_relu")
        delta_step = sem("delta_steps")
        sp_exp = sem("softplus_exp")
        sp_ln = sem("softplus_ln")
        delta_done = sem("delta_done")
        skip_done = sem("skip_done")
        du_done = sem("du_done")
        decay_done = sem("decay_done")
        input_dve = sem("input_dve")
        input_pool = sem("input_pool")
        scan_done = sem("scan_done")
        read_done = sem("readout_done")
        yacc_done = sem("yacc_done")
        skip_acc = sem("skip_accumulated")
        gT_done = sem("gT_done")
        g_tr = sem("g_transposed")
        g_done = sem("g_done")
        oproj_done = sem("oproj_done")
        gated_done = sem("gated_done")
        x1_done = sem("x1_done")
        bn2_done = sem("bn2_done")
        stats2_done = sem("stats2_done")
        rstd2_eps = sem("rstd2_eps")
        rstd2_done = sem("rstd2_done")
        xhat2_done = sem("xhat2_done")
        x1T_done = sem("x1T_done")
        h2_done = sem("h2_done")
        router_mm = sem("router_matmul")
        lg_step = sem("router_logits_steps")
        router_exp = sem("router_exp")
        prob_step = sem("router_prob_steps")
        w9_done = sem("weights_done")
        w9T_mm = sem("weights_transposed")
        w9T_done = sem("weightsT_done")
        up_done = sem("up_done")
        gelu_done = sem("gelu_done")
        down_done = sem("down_done")
        mixmul_done = sem("mixmul_done")
        mixsum_done = sem("mixsum_done")
        fin_step = sem("final_steps")
        out_done = sem("out_done")

        block = ctx.enter_context(nc.Block())

        def chunks_after(b, c):
            return b.i * CH + (c + 1)

        pool_inputs = len(POOL_INPUT_CHUNKS)
        dve_inputs = CH - pool_inputs

        def inputs_after(b, c):
            if c in POOL_INPUT_CHUNKS:
                return input_pool, b.i * pool_inputs + POOL_INPUT_CHUNKS.index(c) + 1
            return input_dve, b.i * dve_inputs + len([k for k in range(c + 1)
                                                      if k not in POOL_INPUT_CHUNKS])

        CONSTS = 8
        SET_LOADS = 22 * 16

        def pipeline(eng, slots):
            slots(None, None, Batch(0, 0))
            slots(Batch(0, 0), None, Batch(1, 1))
            slots(Batch(1, 1), Batch(0, 0), Batch(2, 0))
            with eng.Fori(2, B - 2, 2) as i:
                slots(Batch(i, 0), Batch(i - 1, 1), Batch(i + 1, 1))
                slots(Batch(i + 1, 1), Batch(i, 0), Batch(i + 2, 0))
            slots(Batch(B - 2, 0), Batch(B - 3, 1), Batch(B - 1, 1))
            slots(Batch(B - 1, 1), Batch(B - 2, 0), None)
            slots(None, Batch(B - 1, 1), None)

        @block.sync
        def _(sp):
            loads = [
                (in_raw, in_proj_w.rearrange("(j p) d -> p j d", p=P)),
                (conv_raw, conv_w.rearrange("(q p) o k -> p q (o k)", p=P)),
                (vec_raw[ROW_RB1:ROW_SB1, :], rb1.rearrange("e (q p) -> (e q) p", p=P)),
                (vec_raw[ROW_SB1:ROW_CONVB, :], sb1.rearrange("(q p) -> q p", p=P)),
                (vec_raw[ROW_CONVB:ROW_DTB, :], conv_b.rearrange("(q p) -> q p", p=P)),
                (vec_raw[ROW_DTB:ROW_D, :], dt_b.rearrange("(q p) -> q p", p=P)),
                (vec_raw[ROW_D:ROWS, :], d_skip.rearrange("(q p) -> q p", p=P)),
                (cond_raw, cond),
                (xp_raw[0:2 * NS, :], x_proj_w[R:R + 2 * NS, :]),
                (xp_raw[2 * NS:2 * NS + R, :], x_proj_w[0:R, :]),
                (a_raw, a_log.rearrange("(q p) n -> p q n", p=P)),
                (wmod_sb, wmod),
                (out_raw, out_proj_w),
                (router_sb[:, :], router_w),
                (router_bias[:, :], router_b.partition_broadcast(P)),
                (up_w[:, 0:E, :], rw1.rearrange("e d h -> d e h")),
                (up_w[:, E, :], sw1),
                (down_w[:, 0:E, :, :], rw2.rearrange("e (q p) d -> p e q d", p=P)),
                (down_w[:, E, :, :], sw2.rearrange("(q p) d -> p q d", p=P)),
                (down_bias[0:E, :], rb2),
                (down_bias[E:E + 1, :], sb2.rearrange("(a d) -> a d", a=1)),
            ]
            sp.dma_start(x_sb[:, :, :], x[0].rearrange("(t p) d -> p t d", p=P)).then_inc(x_in, 16)
            for dst, src in loads:
                sp.dma_start(dst, src).then_inc(w_in, 16)
            sp.wait_ge(const_made, CONSTS)
            sp.dma_start(dt_raw[:, :, 2 * NS:2 * NS + R],
                         dt_w.rearrange("(q p) r -> p q r", p=P)).then_inc(w_in, 16)
            sp.wait_ge(gate_steps, 4)
            sp.dma_start(gate_dram, gate_raw).then_inc(gates_stored, 16)
            sp.wait_ge(gates_stored, 16)

            def load_bc(b, pair):
                if not (isinstance(b.i, int) and b.i * NC + pair < BC_RING):
                    sp.wait_ge(read_done, b.i * CH + Q * (pair - BC_RING + 1))
                for which in range(2):
                    src = bc_dram[b.i, which * NS + pair * NG:which * NS + (pair + 1) * NG, :]
                    sp.dma_start(bc[:, pair % BC_RING, which, :, :].rearrange("p n t -> p (n t)"),
                                 src.rearrange("n t -> (n t)").partition_broadcast(P)
                                 ).then_inc(bc_in[pair % BC_RING], 16)

            def slots(b, a, n):
                if n and not (isinstance(n.i, int) and n.i == 0):
                    sp.wait_ge(xT_done, n.i)
                    sp.dma_start(x_sb[:, :, :],
                                 x[n.i].rearrange("(t p) d -> p t d", p=P)).then_inc(x_in, 16)
                if b:
                    load_bc(b, 2)
                if n:
                    sp.wait_ge(bcdt_done, n.i + 1)
                    sp.dma_start(bc_dram[n.i], bcdt[0:2 * NS, :]).then_inc(bc_stored, 16)
                if b:
                    load_bc(b, 3)
                if n:
                    sp.wait_ge(bc_stored, n.i * 16 + 16)
                    load_bc(n, 0)
                if a:
                    sp.wait_ge(out_done, a.i + 1)
                    sp.dma_start(out[a.i].rearrange("(t p) d -> p t d", p=P),
                                 out_sb[:, :, :]).then_inc(out_stored, 16)
                if b:
                    sp.dma_start(x1[:, :, :],
                                 x[b.i].rearrange("(t p) d -> p t d", p=P)).then_inc(x1_in, 16)
                    sp.dma_start(gates[:, :, :].rearrange("p g d -> p (g d)"),
                                 gate_dram[b.i].partition_broadcast(P)).then_inc(x1_in, 16)
                if n:
                    load_bc(n, 1)

            pipeline(sp, slots)
            sp.wait_ge(out_stored, 16 * B)

        @block.gpsimd
        def _(pool):
            pool.memset(ident[:, :], 0.0).then_inc(const_made, 1)
            pool.memset(before[:, :, :], 1.0).then_inc(const_made, 1)
            pool.memset(minus_half, -0.5).then_inc(const_made, 1)
            pool.memset(eps_tile, EPS).then_inc(const_made, 1)
            pool.memset(dt_raw, 0.0).then_inc(const_made, 1)
            pool.memset(w9[:, :, :], 1.0).then_inc(const_made, 1)
            pool.wait_ge(const_made, 6)
            pool.affine_select(out=ident[:, :], in_=ident[:, :], pattern=[[-1, P]],
                               compare_op=ALU.not_equal, fill=1.0, base=0,
                               channel_multiplier=1).then_inc(const_made, 1)
            pool.affine_select(out=before[:, :, :], in_=before[:, :, :], pattern=[[1, E], [-1, E]],
                               compare_op=ALU.is_gt, fill=0.0, base=0,
                               channel_multiplier=0).then_inc(const_made, 1)

            def make_rstd(which, stats, eps_added, done, b):
                pool.wait_ge(stats, b.i + 1)
                pool.tensor_tensor(rstd[:, which, :], mean_var[:, which, :, 1], eps_tile,
                                   ALU.add).then_inc(eps_added, 1)
                pool.wait_ge(eps_added, b.i + 1)
                pool.tensor_tensor(rstd[:, which, :], rstd[:, which, :], minus_half,
                                   ALU.pow).then_inc(done, 1)

            def scan_input(b, c):
                if c in POOL_INPUT_CHUNKS:
                    pair, q = c // Q, c % Q
                    pool.wait_ge(bc_in[pair % BC_RING], b.i * 64 + 32 * (pair // BC_RING + 1))
                    if not (isinstance(b.i, int) and b.i == 0 and c < STATE_RING):
                        pool.wait_ge(yacc_done, chunks_after(b, c - STATE_RING))
                    pool.tensor_tensor(state[:, c % STATE_RING, :, :], bc[:, pair % BC_RING, 0, :, :],
                                       du[:, b.p, q:q + 1, :].broadcast_to([P, NG, L]),
                                       ALU.mult).then_inc(input_pool, 1)

            def readout(b, c):
                pair = c // Q
                pool.wait_ge(scan_done, chunks_after(b, c))
                pool.tensor_tensor(state[:, c % STATE_RING, :, :], state[:, c % STATE_RING, :, :],
                                   bc[:, pair % BC_RING, 1, :, :], ALU.mult).then_inc(read_done, 1)

            def delta_x(n):
                pool.wait_ge(delta_done, Q * n.i + Q)
                pool.wait_ge(xproj_done, n.i + 1)
                pool.wait_ge(skip_done, Q * n.i + Q)
                pool.tensor_tensor(du[:, n.p, :, :], du[:, n.p, :, :], delta[:, n.p, :, :],
                                   ALU.mult).then_inc(du_done, 1)

            pool.wait_ge(setup_done, 1)

            def slots(b, a, n):
                if n:
                    make_rstd(0, stats_done, rstd_eps, rstd_done, n)
                for c in range(CH):
                    if b:
                        if c == 0:
                            scan_input(b, 0)
                        if c + 1 < CH:
                            scan_input(b, c + 1)
                        readout(b, c)
                    if a and c == 1:
                        make_rstd(1, stats2_done, rstd2_eps, rstd2_done, a)
                    if n and c == 4:
                        delta_x(n)

            pipeline(pool, slots)


        @block.tensor
        def _(pe):
            pe.wait_ge(const_made, CONSTS)
            pe.wait_ge(w_in, SET_LOADS)
            pe.wait_ge(raw_ready, 1)
            for q in range(Q):
                for k in range(KC):
                    nc.tensor.transpose(psum[:, q, k * P:(k + 1) * P], conv_in_raw[:, q, k, :],
                                        ident[:, :])
            for q in range(Q):
                nc.tensor.transpose(psum[:, 2, q * P:(q + 1) * P], in_raw[:, Q + q, :], ident[:, :])
                nc.tensor.transpose(psum[:, 3, q * 64:q * 64 + 2 * NS + R],
                                    xp_raw[:, q * P:(q + 1) * P], ident[0:2 * NS + R, 0:2 * NS + R])
                nc.tensor.transpose(psum[:, 4, q * P:(q + 1) * P], out_raw[:, q * P:(q + 1) * P],
                                    ident[:, :])
                nc.tensor.transpose(psum[0:2 * NS + R, 5, q * P:(q + 1) * P], dt_raw[:, q, :],
                                    ident[:, :])
            nc.tensor.transpose(psum[:, 6, 0:ROWS], vec_raw, ident[0:ROWS, 0:ROWS])
            nc.tensor.transpose(psum[:, 7, 448:448 + B], cond_raw,
                                ident[0:B, 0:B]).then_inc(set_mm, 1)
            pe.wait_ge(cond_silu, 1)
            for j, chunk in enumerate((SA, CA, SB, CB)):
                nc.tensor.matmul(psum[:, 7, j * B:(j + 1) * B], wmod_sb[:, chunk * DM:(chunk + 1) * DM],
                                 condT, start=True, stop=True)
            for j, chunk in enumerate((GA, GB)):
                last = nc.tensor.matmul(psum[0:B, 7, 128 + j * DM:128 + (j + 1) * DM], condT,
                                        wmod_sb[:, chunk * DM:(chunk + 1) * DM], start=True, stop=True)
            last.then_inc(set_mm, 1)
            pe.wait_ge(setup_done, 1)

            def y_start(b):
                if not (isinstance(b.i, int) and b.i == 0):
                    pe.wait_ge(gT_done, b.i)
                pe.wait_ge(skip_done, Q * b.i + Q)
                for q in range(Q):
                    for t in range(NT):
                        last = nc.tensor.matmul(Y[q][:, t * P:(t + 1) * P],
                                                skip[:, q, t * P:(t + 1) * P], ident[:, :],
                                                start=(t == 0), stop=False, is_transpose=True,
                                                skip_group_check=True)
                last.then_inc(skip_acc, 1)

            def y_add(b, c):
                q = c % Q
                pe.wait_ge(read_done, chunks_after(b, c))
                for s in range(NG):
                    for t in range(NT):
                        last = nc.tensor.matmul(Y[q][:, t * P:(t + 1) * P],
                                                state[:, c % STATE_RING, s, t * P:(t + 1) * P],
                                                ident[:, :], start=False,
                                                stop=(c >= CH - Q and s == NG - 1),
                                                is_transpose=True, skip_group_check=True)
                last.then_inc(yacc_done, 1)

            def x_transpose(n, a):
                pe.wait_ge(xhat_done, n.i + 1)
                if not (isinstance(n.i, int) and n.i == 0):
                    pe.wait_ge(bcdt_done, n.i)
                if not (isinstance(n.i, int) and n.i < 3):
                    pe.wait_ge(w9T_done, n.i - 2)
                for t in range(NT):
                    last = nc.tensor.transpose(MISC[:, t * P:(t + 1) * P], x_sb[:, t, :], ident[:, :])
                last.then_inc(xT_done, 1)

            def conv_in(n):
                pe.wait_ge(h_done, n.i + 1)
                if not (isinstance(n.i, int) and n.i == 0):
                    pe.wait_ge(delta_done, Q * n.i)
                if not (isinstance(n.i, int) and n.i < 3):
                    pe.wait_ge(gelu_done, M_UP * (n.i - 2))
                for q in range(Q):
                    for k in range(KC):
                        last = nc.tensor.matmul(WORK[q], conv_in_wT[:, q, k, :], h_sb[:, k:k + L],
                                                start=(k == 0), stop=(k == KC - 1))
                    last.then_inc(conv_done, 1)

            def z_proj(n, a):
                if a:
                    pe.wait_ge(g_done, a.i + 1)
                elif n.i > 0:
                    pe.wait_ge(zs_done, 2 * n.i)
                for t in range(NT):
                    last = nc.tensor.matmul(WIDE[:, t * DI:(t + 1) * DI],
                                            h_sb[:, KC - 1 + t * P:KC - 1 + (t + 1) * P],
                                            z_wT[:, :], start=True, stop=True)
                last.then_inc(z_done, 1)

            def x_proj(n, a):
                pe.wait_ge(xb_done, Q * n.i + Q)
                if a:
                    pe.wait_ge(h2_done, a.i + 1)
                else:
                    pe.wait_ge(h_done, n.i + 1)
                for q in range(Q):
                    last = nc.tensor.matmul(MISC[0:2 * NS + R, :], xp_wT[:, q, :], du[:, n.p, q, :],
                                            start=(q == 0), stop=(q == Q - 1))
                last.then_inc(xproj_done, 1)

            def dt_proj(n):
                pe.wait_ge(bcdt_done, n.i + 1)
                for q in range(Q):
                    nc.tensor.matmul(WORK[q], dt_wT[2 * NS:2 * NS + R, q, :],
                                     bcdt[2 * NS:2 * NS + R, :], start=True,
                                     stop=True).then_inc(dt_done, 1)

            def g_transpose(a):
                pe.wait_ge(gT_done, a.i + 1)
                if not (isinstance(a.i, int) and a.i == 0):
                    pe.wait_ge(mixmul_done, NT * a.i)
                last_batch = isinstance(a.i, int) and a.i == B - 1
                pe.wait_ge(zs_done, 2 * B if last_batch else 2 * a.i + 4)
                for q in range(Q):
                    for t in range(NT):
                        last = nc.tensor.transpose(WIDE[:, q * L + t * P:q * L + (t + 1) * P],
                                                   gT[:, t, q * P:(q + 1) * P], ident[:, :])
                last.then_inc(g_tr, 1)

            def out_proj(a):
                pe.wait_ge(g_done, a.i + 1)
                if not (isinstance(a.i, int) and a.i == 0):
                    pe.wait_ge(fin_step, 2 * a.i)
                for t in range(NT):
                    for q in range(Q):
                        last = nc.tensor.matmul(OUTP[:, t * DM:(t + 1) * DM],
                                                g_soft[:, q, t * P:(t + 1) * P], out_wT[:, q, :],
                                                start=(q == 0), stop=(q == Q - 1))
                last.then_inc(oproj_done, 1)

            def x1_transpose(a, n):
                pe.wait_ge(xhat2_done, a.i + 1)
                if n:
                    pe.wait_ge(h_done, n.i + 1)
                else:
                    pe.wait_ge(w9T_done, a.i)
                for t in range(NT):
                    last = nc.tensor.transpose(MISC[:, t * P:(t + 1) * P], xhat2[:, t, :], ident[:, :])
                last.then_inc(x1T_done, 1)

            def router(a, n):
                pe.wait_ge(h2_done, a.i + 1)
                if n:
                    pe.wait_ge(bcdt_done, n.i + 1)
                for t in range(NT):
                    last = nc.tensor.matmul(MISC[:, t * E:(t + 1) * E], h2[:, t * P:(t + 1) * P],
                                            router_sb[:, :], start=True, stop=True)
                last.then_inc(router_mm, 1)

            def up(a, n, m):
                if m == 0:
                    pe.wait_ge(h2_done, a.i + 1)
                if m >= 2:
                    pe.wait_ge(gelu_done, M_UP * a.i + m - 1)
                elif n:
                    pe.wait_ge(delta_done, Q * n.i + m + 1)
                elif not (isinstance(a.i, int) and a.i == 0):
                    pe.wait_ge(gelu_done, M_UP * a.i)
                nc.tensor.matmul(WORK[m % 2], up_w[:, m // HQ, (m % HQ) * P:(m % HQ + 1) * P],
                                 h2[:, :], start=True, stop=True).then_inc(up_done, 1)

            def weights_transpose(a):
                pe.wait_ge(w9_done, a.i + 1)
                pe.wait_ge(lg_step, 3 * a.i + 1)
                for t in range(NT):
                    last = nc.tensor.transpose(MISC[0:E + 1, t * P:(t + 1) * P], w9[:, t, :],
                                               ident[:, :])
                last.then_inc(w9T_mm, 1)

            def down(a, n, t):
                if t == 0:
                    pe.wait_ge(gelu_done, M_UP * a.i + M_UP)
                    pe.wait_ge(w9T_done, a.i + 1)
                    pe.wait_ge(gated_done, a.i + 1)
                    if n:
                        pe.wait_ge(zs_done, 2 * n.i + 2)
                    else:
                        pe.wait_ge(g_done, a.i + 1)
                else:
                    pe.wait_ge(mixmul_done, NT * a.i + t)
                ts = slice(t * P, (t + 1) * P)
                for e in range(E):
                    for q in range(HQ):
                        nc.tensor.matmul(WIDE[:, e * DM:(e + 1) * DM], h1[:, e * HQ + q, ts],
                                         down_w[:, e, q, :], start=(q == 0), stop=(q == HQ - 1))
                for q in range(HQ):
                    nc.tensor.matmul(OUTP[:, ts], h1[:, E * HQ + q, ts], down_w[:, E, q, :],
                                     start=(q == 0), stop=False)
                nc.tensor.matmul(OUTP[:, ts], w9T[:, ts], down_bias[:, :], start=False,
                                 stop=True).then_inc(down_done, 1)

            def slots(b, a, n):
                if a:
                    y_add(a, CH - 1)
                if n:
                    x_transpose(n, a)
                if a:
                    g_transpose(a)
                if b:
                    y_start(b)
                if n:
                    conv_in(n)
                if a:
                    out_proj(a)
                if n:
                    z_proj(n, a)
                if b:
                    y_add(b, 0)
                if a:
                    x1_transpose(a, n)
                if b:
                    y_add(b, 1)
                if n:
                    x_proj(n, a)
                if a:
                    router(a, n)
                if n:
                    dt_proj(n)
                if b:
                    y_add(b, 2)
                for m in range(M_UP):
                    if a:
                        up(a, n, m)
                    if b and m == 8:
                        y_add(b, 3)
                if a:
                    weights_transpose(a)
                if b:
                    y_add(b, 4)
                for t in range(NT):
                    if a:
                        down(a, n, t)
                    if b and t in (1, 3):
                        y_add(b, 5 + t // 2)

            pipeline(pe, slots)

        @block.scalar
        def _(act):
            act.wait_ge(w_in, SET_LOADS)
            nc.scalar.activation(a_neg[:, :, :], a_raw, ACT.Exp).then_inc(a_exp, 1)
            act.wait_ge(set_mm, 1)
            nc.scalar.activation(condT, psum[:, 7, 448:448 + B], ACT.Silu).then_inc(cond_silu, 1)
            act.wait_ge(setup_done, 1)

            def decays(b, c):
                pair, q = c // Q, c % Q
                r = c % DECAY_RING
                if c == 0:
                    act.wait_ge(delta_done, Q * b.i + Q)
                if not (isinstance(b.i, int) and b.i == 0 and c < DECAY_RING):
                    act.wait_ge(scan_done, chunks_after(b, c - DECAY_RING))
                for s in range(NG):
                    k = pair * NG + s
                    last = nc.scalar.activation(decay[:, r, s, 1:L], delta[:, b.p, q, 1:L], ACT.Exp,
                                                scale=a_neg[:, q, k:k + 1])
                last.then_inc(decay_done, 1)

            def h_rows(n):
                act.wait_ge(xT_done, n.i + 1)
                if not (isinstance(n.i, int) and n.i == 0):
                    act.wait_ge(z_done, n.i)
                nc.scalar.activation(h_sb[:, KC - 1:KC - 1 + L], MISC, ACT.Identity,
                                     scale=modT[:, 1, bass.ds(n.i, 1)],
                                     bias=modT[:, 0, bass.ds(n.i, 1)]).then_inc(h_done, 1)

            def x_silu(n):
                if not (isinstance(n.i, int) and n.i < 2):
                    act.wait_ge(scan_done, (n.i - 1) * CH)
                for q in range(Q):
                    act.wait_ge(conv_done, Q * n.i + q + 1)
                    nc.scalar.activation(du[:, n.p, q, :], WORK[q], ACT.Silu,
                                         bias=vec[:, ROW_CONVB + q:ROW_CONVB + q + 1]
                                         ).then_inc(xb_done, 1)

            def skip_term(n):
                if not (isinstance(n.i, int) and n.i == 0):
                    act.wait_ge(skip_acc, n.i)
                for q in range(Q):
                    act.wait_ge(xb_done, Q * n.i + q + 1)
                    nc.scalar.activation(skip[:, q, :], du[:, n.p, q, :], ACT.Identity,
                                         scale=vec[:, ROW_D + q:ROW_D + q + 1]).then_inc(skip_done, 1)

            def z_gate(n):
                act.wait_ge(z_done, n.i + 1)
                if not (isinstance(n.i, int) and n.i < 2):
                    act.wait_ge(gT_done, n.i - 1)
                zs = z_silu[:, n.p, :, :].rearrange("p t c -> p (t c)")
                for j in range(2):
                    nc.scalar.activation(zs[:, j * 512:(j + 1) * 512], WIDE[:, j * 512:(j + 1) * 512],
                                         ACT.Silu).then_inc(zs_done, 1)

            def bcdt_rows(n):
                act.wait_ge(xproj_done, n.i + 1)
                if not (isinstance(n.i, int) and n.i == 0):
                    act.wait_ge(bc_stored, n.i * 16)
                    act.wait_ge(dt_done, Q * n.i)
                nc.scalar.activation(bcdt[:, :], MISC[0:2 * NS + R, :], ACT.Copy).then_inc(bcdt_done, 1)

            def softplus(n, a):
                if a:
                    act.wait_ge(oproj_done, a.i + 1)
                for q in range(Q):
                    bias = vec[:, ROW_DTB + q:ROW_DTB + q + 1]
                    act.wait_ge(dt_done, Q * n.i + q + 1)
                    nc.scalar.activation(g_soft[:, q, :], WORK[q], ACT.Abs,
                                         bias=bias).then_inc(sp_abs, 1)
                    nc.scalar.activation(delta[:, n.p, q, :], WORK[q], ACT.Relu,
                                         bias=bias).then_inc(sp_relu, 1)
                act.wait_ge(sp_abs, Q * n.i + Q)
                nc.scalar.activation(g_soft[:, :, :], g_soft[:, :, :], ACT.Exp,
                                     scale=-1.0).then_inc(sp_exp, 1)
                act.wait_ge(sp_exp, n.i + 1)
                act.wait_ge(sp_relu, Q * n.i + Q)
                nc.scalar.activation(psum[:, 2:4, :], g_soft[:, :, :], ACT.Ln,
                                     bias=1.0).then_inc(sp_ln, 1)

            def g_rows(a, n):
                act.wait_ge(g_tr, a.i + 1)
                act.wait_ge(delta_done, Q * a.i + 2 * Q if n or isinstance(a.i, int) and a.i < B - 1
                            else Q * B)
                nc.scalar.activation(g_soft[:, :, :].rearrange("p q t -> p (q t)"), WIDE,
                                     ACT.Copy).then_inc(g_done, 1)

            def h2_rows(a):
                act.wait_ge(x1T_done, a.i + 1)
                if not (isinstance(a.i, int) and a.i == 0):
                    act.wait_ge(up_done, M_UP * a.i)
                nc.scalar.activation(h2[:, :], MISC, ACT.Identity, scale=modT[:, 3, bass.ds(a.i, 1)],
                                     bias=modT[:, 2, bass.ds(a.i, 1)]).then_inc(h2_done, 1)

            def router_e(a):
                act.wait_ge(lg_step, 3 * a.i + 3)
                nc.scalar.activation(ex[:, :, :], lg[:, :, :], ACT.Exp).then_inc(router_exp, 1)

            def gelu(a, m):
                act.wait_ge(up_done, M_UP * a.i + m + 1)
                if m == 0 and not (isinstance(a.i, int) and a.i == 0):
                    act.wait_ge(down_done, NT * a.i)
                bias = ROW_RB1 + m
                nc.scalar.activation(h1[:, m, :], WORK[m % 2], ACT.Gelu,
                                     bias=vec[:, bias:bias + 1]).then_inc(gelu_done, 1)

            def slots(b, a, n):
                if n:
                    h_rows(n)
                if b:
                    decays(b, 2)
                if a:
                    g_rows(a, n)
                if b:
                    decays(b, 3)
                if n:
                    x_silu(n)
                    z_gate(n)
                    skip_term(n)
                if a:
                    h2_rows(a)
                if n:
                    bcdt_rows(n)
                if b:
                    decays(b, 4)
                if a:
                    router_e(a)
                if n:
                    softplus(n, a)
                if b:
                    decays(b, 5)
                if a:
                    for m in range(M_UP):
                        gelu(a, m)
                if b:
                    decays(b, 6)
                    decays(b, 7)
                if n:
                    decays(n, 0)
                    decays(n, 1)

            pipeline(act, slots)

        @block.vector
        def _(dve):
            nc.vector.memset(h_sb[:, 0:KC - 1], 0.0)
            nc.vector.memset(decay[:, :, :, 0:1], 0.0)
            dve.wait_ge(w_in, SET_LOADS)
            for q in range(Q):
                for k in range(KC):
                    last = nc.vector.tensor_scalar(conv_in_raw[:, q, k, :], in_raw[:, q, :],
                                                   conv_raw[:, q, k:k + 1], None, ALU.mult)
            last.then_inc(raw_ready, 1)
            dve.wait_ge(set_mm, 1)
            for q in range(Q):
                nc.vector.tensor_copy(conv_in_wT[:, q, :, :].rearrange("p k c -> p (k c)"),
                                      psum[:, q, :])
                nc.vector.tensor_copy(xp_wT[:, q, :], psum[:, 3, q * 64:q * 64 + 2 * NS + R])
            nc.vector.tensor_copy(z_wT[:, :], psum[:, 2, 0:DI])
            nc.vector.tensor_copy(out_wT[:, :, :].rearrange("p q d -> p (q d)"), psum[:, 4, 0:DI])
            nc.vector.tensor_copy(small_w[0:2 * NS + R, :],
                                  psum[0:2 * NS + R, 5, 0:Q * P])
            nc.vector.tensor_copy(vec[:, :], psum[:, 6, 0:ROWS])
            dve.wait_ge(a_exp, 1)
            nc.vector.tensor_scalar(a_neg[:, :, :], a_neg[:, :, :], -1.0, None, ALU.mult)
            dve.wait_ge(set_mm, 2)
            for j in range(4):
                nc.vector.tensor_scalar(modT[:, j, :], psum[:, 7, j * B:(j + 1) * B],
                                        float(j % 2), None, ALU.add)
            gate_ps = psum[0:B, 7, 128:128 + 2 * DM]
            nc.vector.tensor_scalar(gate_sign, gate_ps, 0.0, 2.0, ALU.is_ge,
                                    ALU.mult).then_inc(gate_steps, 1)
            nc.vector.tensor_scalar(gate_abs, gate_ps, -1.0, GATE_MIN, ALU.mult,
                                    ALU.max).then_inc(gate_steps, 1)
            dve.wait_ge(gate_steps, 2)
            nc.vector.tensor_tensor(gate_abs, gate_abs, gate_ps, ALU.max).then_inc(gate_steps, 1)
            dve.wait_ge(gate_steps, 3)
            nc.vector.scalar_tensor_tensor(out=gate_raw, in0=gate_sign, scalar=-1.0, in1=gate_abs,
                                           op0=ALU.add, op1=ALU.mult).then_inc(gate_steps, 1)
            dve.wait_ge(gates_stored, 16)
            nc.vector.memset(rsum, 0.0).then_inc(setup_done, 1)

            def stats(n):
                dve.wait_ge(x_in, 16 * n.i + 16)
                for t in range(NT):
                    last = nc.vector.bn_stats(bn[:, t, :], x_sb[:, t, :])
                last.then_inc(bn_done, 1)
                dve.wait_ge(bn_done, n.i + 1)
                nc.vector.memset(pace, 0.0)
                for t in range(NT):
                    last = nc.vector.bn_aggr(mean_var[:, 0, t, :], bn[:, t, :])
                last.then_inc(stats_done, 1)

            def xhat(n):
                dve.wait_ge(rstd_done, n.i + 1)
                for t in range(NT):
                    last = nc.vector.tensor_scalar(x_sb[:, t, :], x_sb[:, t, :],
                                                   mean_var[:, 0, t, 0:1], rstd[:, 0, t:t + 1],
                                                   ALU.subtract, ALU.mult)
                last.then_inc(xhat_done, 1)

            def make_delta(n):
                work = psum[:, 2:4, :]
                d = delta[:, n.p, :, :]
                dve.wait_ge(sp_ln, n.i + 1)
                nc.vector.tensor_tensor(d, d, work, ALU.add).then_inc(delta_step, 1)
                dve.wait_ge(delta_step, 3 * n.i + 1)
                nc.vector.tensor_scalar(work, g_soft[:, :, :], 1.0, 1.0, ALU.add,
                                        ALU.subtract).then_inc(delta_step, 1)
                nc.vector.tensor_tensor(d, d, g_soft[:, :, :], ALU.add).then_inc(delta_step, 1)
                dve.wait_ge(delta_step, 3 * n.i + 3)
                for q in range(Q):
                    nc.vector.tensor_tensor(delta[:, n.p, q, :], delta[:, n.p, q, :], WORK[q],
                                            ALU.subtract).then_inc(delta_done, 1)

            def scan_input(b, c):
                if c not in POOL_INPUT_CHUNKS:
                    pair, q = c // Q, c % Q
                    if c == 0:
                        dve.wait_ge(du_done, b.i + 1)
                    dve.wait_ge(bc_in[pair % BC_RING], b.i * 64 + 32 * (pair // BC_RING + 1))
                    if not (isinstance(b.i, int) and b.i == 0 and c < STATE_RING):
                        dve.wait_ge(yacc_done, chunks_after(b, c - STATE_RING))
                    nc.vector.tensor_tensor(state[:, c % STATE_RING, :, :],
                                            bc[:, pair % BC_RING, 0, :, :],
                                            du[:, b.p, q:q + 1, :].broadcast_to([P, NG, L]),
                                            ALU.mult).then_inc(input_dve, 1)

            def scan(b, c):
                scan_input(b, c)
                dve.wait_ge(decay_done, chunks_after(b, c))
                dve.wait_ge(*inputs_after(b, c))
                s = state[:, c % STATE_RING, :, :].rearrange("p n t -> p (n t)")
                nc.vector.tensor_tensor_scan(s, decay[:, c % DECAY_RING, :, :].rearrange(
                    "p n t -> p (n t)"), s, 0.0, ALU.mult, ALU.add).then_inc(scan_done, 1)

            def gate_y(a):
                dve.wait_ge(yacc_done, chunks_after(a, CH - 1))
                dve.wait_ge(zs_done, 2 * a.i + 2)
                if not (isinstance(a.i, int) and a.i == 0):
                    dve.wait_ge(mixsum_done, NT * a.i)
                nc.vector.tensor_tensor(
                    gT.rearrange("p t (q c) -> p q t c", q=Q),
                    psum[:, 0:2, :].rearrange("p q (t c) -> p q t c", t=NT),
                    z_silu[:, a.p, :, :].rearrange("p t (q c) -> p q t c", q=Q),
                    ALU.mult).then_inc(gT_done, 1)

            def residual(a):
                dve.wait_ge(oproj_done, a.i + 1)
                dve.wait_ge(x1_in, 32 * a.i + 32)
                if not (isinstance(a.i, int) and a.i == 0):
                    dve.wait_ge(out_stored, 16 * a.i)
                nc.vector.tensor_tensor(out_sb[:, :, :], OUTP.rearrange("p (t d) -> p t d", t=NT),
                                        gates[:, 0:1, :].broadcast_to([P, NT, DM]),
                                        ALU.mult).then_inc(gated_done, 1)
                dve.wait_ge(gated_done, a.i + 1)
                nc.vector.tensor_tensor(x1[:, :, :], x1[:, :, :], out_sb[:, :, :],
                                        ALU.add).then_inc(x1_done, 1)
                dve.wait_ge(x1_done, a.i + 1)
                for t in range(NT):
                    last = nc.vector.bn_stats(bn[:, t, :], x1[:, t, :])
                last.then_inc(bn2_done, 1)
                dve.wait_ge(bn2_done, a.i + 1)
                nc.vector.memset(pace, 0.0)
                for t in range(NT):
                    last = nc.vector.bn_aggr(mean_var[:, 1, t, :], bn[:, t, :])
                last.then_inc(stats2_done, 1)

            def x1hat(a):
                dve.wait_ge(rstd2_done, a.i + 1)
                for t in range(NT):
                    last = nc.vector.tensor_scalar(xhat2[:, t, :], x1[:, t, :],
                                                   mean_var[:, 1, t, 0:1], rstd[:, 1, t:t + 1],
                                                   ALU.subtract, ALU.mult)
                last.then_inc(xhat2_done, 1)

            def logits(a):
                dve.wait_ge(router_mm, a.i + 1)
                dve.wait_ge(g_tr, a.i + 1)
                nc.vector.tensor_tensor(lg[:, :, :], MISC[:, 0:NT * E].rearrange("p (t e) -> p t e", t=NT),
                                        router_bias[:, :].unsqueeze(1).broadcast_to([P, NT, E]),
                                        ALU.add).then_inc(lg_step, 1)
                dve.wait_ge(lg_step, 3 * a.i + 1)
                nc.vector.tensor_reduce(rmax, lg[:, :, :], AX.X, ALU.max).then_inc(lg_step, 1)
                dve.wait_ge(lg_step, 3 * a.i + 2)
                nc.vector.tensor_tensor(lg[:, :, :], lg[:, :, :],
                                        rmax.unsqueeze(2).broadcast_to([P, NT, E]),
                                        ALU.subtract).then_inc(lg_step, 1)

            def top2(a):
                k = 8 * a.i
                dve.wait_ge(router_exp, a.i + 1)
                nc.vector.tensor_reduce(rsum, ex[:, :, :], AX.X, ALU.add).then_inc(prob_step, 1)
                dve.wait_ge(prob_step, k + 1)
                nc.vector.reciprocal(rmax, rsum).then_inc(prob_step, 1)
                dve.wait_ge(prob_step, k + 2)
                nc.vector.tensor_tensor(pr[:, :, :], ex[:, :, :],
                                        rmax.unsqueeze(2).broadcast_to([P, NT, E]),
                                        ALU.mult).then_inc(prob_step, 1)
                dve.wait_ge(prob_step, k + 3)
                mine = pr[:, :, :].unsqueeze(3).broadcast_to([P, NT, E, E])
                other = pr[:, :, :].unsqueeze(2).broadcast_to([P, NT, E, E])
                nc.vector.tensor_tensor(gt_eq[:, 1, :, :, :], other, mine, ALU.is_equal
                                        ).then_inc(prob_step, 1)
                nc.vector.tensor_tensor(gt_eq[:, 0, :, :, :], other, mine, ALU.is_gt
                                        ).then_inc(prob_step, 1)
                dve.wait_ge(prob_step, k + 5)
                nc.vector.tensor_tensor(
                    gt_eq[:, 1, :, :, :], gt_eq[:, 1, :, :, :],
                    before[:, :, :].unsqueeze(1).broadcast_to([P, NT, E, E]),
                    ALU.mult).then_inc(prob_step, 1)
                dve.wait_ge(prob_step, k + 6)
                nc.vector.tensor_tensor(gt_eq[:, 0, :, :, :], gt_eq[:, 0, :, :, :],
                                        gt_eq[:, 1, :, :, :], ALU.add).then_inc(prob_step, 1)
                dve.wait_ge(prob_step, k + 7)
                nc.vector.tensor_reduce(rank[:, :, :], gt_eq[:, 0, :, :, :], AX.X,
                                        ALU.add).then_inc(prob_step, 1)
                dve.wait_ge(prob_step, k + 8)
                nc.vector.scalar_tensor_tensor(out=w9[:, :, 0:E], in0=rank[:, :, :], scalar=1.5,
                                               in1=pr[:, :, :], op0=ALU.is_lt,
                                               op1=ALU.mult).then_inc(w9_done, 1)

            def weights_out(a):
                dve.wait_ge(w9T_mm, a.i + 1)
                if not (isinstance(a.i, int) and a.i == 0):
                    dve.wait_ge(down_done, NT * a.i)
                nc.vector.tensor_copy(w9T[:, :], MISC[0:E + 1, :]).then_inc(w9T_done, 1)

            def mix_block(a, t):
                dve.wait_ge(down_done, NT * a.i + t + 1)
                if t == 0:
                    dve.wait_ge(g_tr, a.i + 1)
                else:
                    dve.wait_ge(mixsum_done, NT * a.i + t)
                nc.vector.tensor_tensor(mix, WIDE.rearrange("p (e d) -> p e d", e=E),
                                        w9[:, t, 0:E].unsqueeze(2).broadcast_to([P, E, DM]),
                                        ALU.mult).then_inc(mixmul_done, 1)
                dve.wait_ge(mixmul_done, NT * a.i + t + 1)
                nc.vector.tensor_reduce(out_sb[:, t, :], mix.rearrange("p e d -> p d e"), AX.X,
                                        ALU.add).then_inc(mixsum_done, 1)

            def finish(a):
                dve.wait_ge(mixsum_done, NT * a.i + NT)
                nc.vector.tensor_tensor(out_sb[:, :, :], out_sb[:, :, :],
                                        OUTP.rearrange("p (t d) -> p t d", t=NT),
                                        ALU.add).then_inc(fin_step, 1)
                dve.wait_ge(fin_step, 2 * a.i + 1)
                nc.vector.tensor_tensor(out_sb[:, :, :], out_sb[:, :, :],
                                        gates[:, 1:2, :].broadcast_to([P, NT, DM]),
                                        ALU.mult).then_inc(fin_step, 1)
                dve.wait_ge(fin_step, 2 * a.i + 2)
                nc.vector.tensor_tensor(out_sb[:, :, :], out_sb[:, :, :], x1[:, :, :],
                                        ALU.add).then_inc(out_done, 1)

            def slots(b, a, n):
                if n:
                    stats(n)
                    xhat(n)
                if b:
                    scan(b, 0)
                if a:
                    gate_y(a)
                if b:
                    scan(b, 1)
                if a:
                    residual(a)
                    x1hat(a)
                if b:
                    scan(b, 2)
                if a:
                    logits(a)
                if b:
                    scan(b, 3)
                if n:
                    make_delta(n)
                if a:
                    top2(a)
                if b:
                    scan(b, 4)
                if a:
                    weights_out(a)
                if b:
                    scan(b, 5)
                for t in range(NT):
                    if a:
                        mix_block(a, t)
                    if b and t in (0, 2):
                        scan(b, 6 + t // 2)
                if a:
                    finish(a)

            pipeline(dve, slots)


_INS = ["L0_attn_hidden_states", "L0_attn_in_proj_w", "L0_attn_conv_w", "L0_attn_conv_b",
        "L0_attn_x_proj_w", "L0_attn_dt_w", "L0_attn_dt_b", "L0_attn_A_log", "L0_attn_D",
        "L0_attn_out_proj_w", "L0_ffn_router_w", "L0_ffn_router_b", "L0_ffn_sw1", "L0_ffn_sb1",
        "L0_ffn_sw2", "L0_ffn_sb2", "L0_ffn_rw1", "L0_ffn_rb1", "L0_ffn_rw2", "L0_ffn_rb2",
        "L0_c", "L0_wmod"]
_OUTS = [((B, L, DM), "float32")]


def kernel(**inputs):
    import numpy as _np
    import concourse.bacc as _bacc
    from concourse import mybir as _mybir
    from concourse.bass_utils import run_bass_kernel_spmd as _run

    nc = _bacc.Bacc("TRN2", target_bir_lowering=False, num_devices=1)
    arrays, args = {}, []
    for name in _INS:
        a = _np.ascontiguousarray(inputs[name])
        arrays[f"in_{name}_dram"] = a
        args.append(nc.dram_tensor(f"in_{name}_dram", a.shape, _mybir.dt.from_np(a.dtype),
                                   kind="ExternalInput").ap())
    for i, (shape, dtype) in enumerate(_OUTS):
        dt = _mybir.dt.from_np(_np.dtype(dtype))
        args.append(nc.dram_tensor(f"out_{i}_dram", shape, dt, kind="ExternalOutput").ap())
    adaln_mamba_moe_kernel(nc, *args)
    r = _run(nc, [arrays], core_ids=[0])
    return r.results[0]["out_0_dram"]
```

```python
from contextlib import ExitStack

import concourse.bass as bass
from concourse import mybir

F32 = mybir.dt.float32
ALU = mybir.AluOpType
ACT = mybir.ActivationFunctionType
AX = mybir.AxisListType

B, L, DM = 8, 512, 128
DI = 2 * DM
NS = 16
R = 8
KC = 4
E, H = 8, 256
P = 128
NT = L // P
Q = DI // P
HQ = H // P
NG = 4
NC = NS // NG
CH = NC * Q
M_UP = (E + 1) * HQ
EPS = 1e-5
GATE_MIN = 0.25
STATE_RING = 4
DECAY_RING = 4
BC_RING = 2
POOL_INPUT_CHUNKS = (1, 4, 6)
ROW_RB1, ROW_SB1, ROW_CONVB, ROW_DTB, ROW_D, ROWS = 0, 16, 18, 20, 22, 24
SA, CA, GA, SB, CB, GB = range(6)


class Batch:

    def __init__(self, index, parity):
        self.i = index
        self.p = parity


def adaln_mamba_moe_kernel(nc, x, in_proj_w, conv_w, conv_b, x_proj_w, dt_w, dt_b, a_log, d_skip,
                           out_proj_w, router_w, router_b, sw1, sb1, sw2, sb2, rw1, rb1, rw2, rb2,
                           cond, wmod, out):
    bc_dram = nc.dram_tensor("bc_rows", [B, 2 * NS, L], F32).ap()
    gate_dram = nc.dram_tensor("gate_rows", [B, 2 * DM], F32).ap()

    with ExitStack() as ctx:
        def sb(name, shape, dtype=F32):
            return ctx.enter_context(nc.sbuf_tensor(name, shape, dtype))

        def sem(name):
            return ctx.enter_context(nc.semaphore(name))

        ident = sb("ident", [P, P])
        conv_in_wT = sb("conv_in_wT", [P, Q, KC, P])
        z_wT = sb("z_wT", [P, DI])
        xp_wT = sb("xp_wT", [P, Q, 2 * NS + R])
        small_w = sb("small_w", [P, Q * P])
        out_wT = sb("out_wT", [P, Q, DM])
        router_sb = sb("router_sb", [P, E])
        router_bias = sb("router_bias", [P, E])
        up_w = sb("up_w", [P, E + 1, H])
        down_w = sb("down_w", [P, E + 1, HQ, DM])
        vec = sb("vec", [P, ROWS])
        a_neg = sb("a_neg", [P, Q, NS])
        modT = sb("modT", [P, 4, B])
        constants = sb("constants", [P, 2 * NT])
        minus_half, eps_tile = constants[:, 0:NT], constants[:, NT:2 * NT]
        before = sb("before", [P, E, E], mybir.dt.bfloat16)
        x_sb = sb("x_sb", [P, NT, DM])
        h_sb = sb("h_sb", [P, KC - 1 + L])
        du = sb("du", [P, 2, Q, L])
        skip = sb("skip", [P, Q, L])
        z_silu = sb("z_silu", [P, 2, NT, DI])
        rows = sb("rows", [P, L])
        delta = sb("delta", [P, 2, Q, L])
        decay = sb("decay", [P, DECAY_RING, NG, L])
        state = sb("state", [P, STATE_RING, NG, L])
        bc = sb("bc", [P, BC_RING, 2, NG, L])
        gT_mix = sb("gT_mix", [P, NT * DI])
        g_soft = sb("g_soft", [P, Q, L])
        x1 = sb("x1", [P, NT, DM])
        gates = sb("gates", [P, 2, DM])
        h2 = sb("h2", [P, L])
        h1 = sb("h1", [P, M_UP, L])
        w9 = sb("w9", [P, NT, E + 1])
        out_sb = sb("out_sb", [P, NT, DM])
        bn = sb("bn", [P, NT, 6])
        mean_var = sb("mean_var", [P, 2, NT, 2])
        rstd = sb("rstd", [P, 2, NT])
        router_stats = sb("router_stats", [P, 2 * NT + 1])
        rmax, rsum = router_stats[:, 0:NT], router_stats[:, NT:2 * NT]
        pace = router_stats[:, 2 * NT:2 * NT + 1]

        gT = gT_mix[:, :].rearrange("p (t c) -> p t c", t=NT)
        mix = gT_mix[:, :].rearrange("p (e d) -> p e d", e=E)
        gt_eq = gT_mix[:, 0:2 * NT * E * E].rearrange("p (g t e j) -> p g t e j", g=2, t=NT, e=E)
        lg, ex, pr, rank = (gT_mix[:, k * NT * E:(k + 1) * NT * E].rearrange("p (t e) -> p t e", t=NT)
                            for k in range(2 * E, 2 * E + 4))
        xhat2 = out_sb
        bcdt = rows[0:2 * NS + R, :]
        w9T = rows[64:64 + E + 1, :]
        dt_wT = small_w[0:2 * NS + R, :].rearrange("p (q d) -> p q d", q=Q)
        down_bias = small_w[64:64 + E + 1, 0:DM]
        raw = state[:, :, :, :].rearrange("p r n t -> p (r n t)")
        in_raw = raw[:, 0:4 * DM].rearrange("p (j d) -> p j d", j=4)
        conv_raw = raw[:, 512:512 + Q * KC].rearrange("p (q k) -> p q k", q=Q)
        conv_in_raw = raw[:, 1024:2048].rearrange("p (q k d) -> p q k d", q=Q, k=KC)
        xp_raw = raw[0:2 * NS + R, 2048:2048 + DI]
        dt_raw = raw[:, 2560:2560 + Q * (2 * NS + R)].rearrange("p (q r) -> p q r", q=Q)
        out_raw = raw[:, 3072:3072 + DI]
        vec_raw = raw[0:ROWS, 3584:3584 + P]
        cond_raw = raw[0:B, 3712:3712 + DM]
        condT = raw[:, 3840:3840 + B]
        a_raw = raw[:, 3904:3904 + Q * NS].rearrange("p (q n) -> p q n", q=Q)
        gate_raw = raw[0:B, 4096:4096 + 2 * DM]
        gate_sign = raw[0:B, 4352:4352 + 2 * DM]
        gate_abs = raw[0:B, 4608:4608 + 2 * DM]
        wmod_sb = raw[:, 5120:5120 + 6 * DM]

        psum = ctx.enter_context(nc.psum_tensor("psum", [P, 8, 512], F32))
        Y = (psum[:, 0, :], psum[:, 1, :])
        WORK = (psum[:, 2, :], psum[:, 3, :])
        WIDE = psum[:, 4:6, :].rearrange("p a c -> p (a c)")
        OUTP = psum[:, 6, :]
        G_ROWS = psum[:, 6:8, :].rearrange("p a c -> p (a c)")
        MISC = psum[:, 7, :]

        w_in = sem("weights_in")
        x_in = sem("x_in")
        x1_in = sem("residual_and_gates_in")
        bc_stored = sem("bc_stored")
        bc_in = [sem(f"bc_in{i}") for i in range(BC_RING)]
        gates_stored = sem("gates_stored")
        out_stored = sem("out_stored")
        const_made = sem("const_made")
        raw_ready = sem("conv_scaled")
        set_mm = sem("setup_matmul")
        set_ev = sem("setup_evacuated")
        cond_silu = sem("cond_silu")
        gate_steps = sem("gate_steps")
        a_exp = sem("a_exp")
        setup_done = sem("setup_done")
        bn_done = sem("bn_done")
        stats_done = sem("stats_done")
        rstd_eps = sem("rstd_eps")
        rstd_done = sem("rstd_done")
        xhat_done = sem("xhat_done")
        xT_done = sem("xT_done")
        h_done = sem("h_done")
        conv_done = sem("conv_done")
        xb_done = sem("xb_done")
        z_done = sem("z_done")
        zs_done = sem("zs_done")
        xproj_done = sem("xproj_done")
        bcdt_done = sem("bcdt_done")
        dt_done = sem("dt_done")
        sp_abs = sem("softplus_abs")
        sp_relu = sem("softplus_relu")
        delta_step = sem("delta_steps")
        sp_exp = sem("softplus_exp")
        sp_ln = sem("softplus_ln")
        delta_done = sem("delta_done")
        skip_done = sem("skip_done")
        du_done = sem("du_done")
        decay_done = sem("decay_done")
        input_dve = sem("input_dve")
        input_pool = sem("input_pool")
        scan_done = sem("scan_done")
        read_done = sem("readout_done")
        yacc_done = sem("yacc_done")
        skip_acc = sem("skip_accumulated")
        gT_done = sem("gT_done")
        g_tr = sem("g_transposed")
        g_done = sem("g_done")
        oproj_done = sem("oproj_done")
        gated_done = sem("gated_done")
        x1_done = sem("x1_done")
        bn2_done = sem("bn2_done")
        stats2_done = sem("stats2_done")
        rstd2_eps = sem("rstd2_eps")
        rstd2_done = sem("rstd2_done")
        xhat2_done = sem("xhat2_done")
        x1T_done = sem("x1T_done")
        h2_done = sem("h2_done")
        router_mm = sem("router_matmul")
        lg_step = sem("router_logits_steps")
        router_exp = sem("router_exp")
        prob_step = sem("router_prob_steps")
        w9_done = sem("weights_done")
        w9T_mm = sem("weights_transposed")
        w9T_done = sem("weightsT_done")
        up_done = sem("up_done")
        gelu_done = sem("gelu_done")
        down_done = sem("down_done")
        mixmul_done = sem("mixmul_done")
        mixsum_done = sem("mixsum_done")
        fin_step = sem("final_steps")
        out_done = sem("out_done")

        block = ctx.enter_context(nc.Block())

        def chunks_after(b, c):
            return b.i * CH + (c + 1)

        pool_inputs = len(POOL_INPUT_CHUNKS)
        dve_inputs = CH - pool_inputs

        def inputs_after(b, c):
            if c in POOL_INPUT_CHUNKS:
                return input_pool, b.i * pool_inputs + POOL_INPUT_CHUNKS.index(c) + 1
            return input_dve, b.i * dve_inputs + len([k for k in range(c + 1)
                                                      if k not in POOL_INPUT_CHUNKS])

        CONSTS = 8
        SET_LOADS = 22 * 16

        def pipeline(eng, slots):
            slots(None, None, None, Batch(0, 0))
            slots(None, None, Batch(0, 0), Batch(1, 1))
            slots(Batch(0, 0), None, Batch(1, 1), Batch(2, 0))
            slots(Batch(1, 1), Batch(0, 0), Batch(2, 0), Batch(3, 1))
            with eng.Fori(2, B - 3, 2) as i:
                slots(Batch(i, 0), Batch(i - 1, 1), Batch(i + 1, 1), Batch(i + 2, 0))
                slots(Batch(i + 1, 1), Batch(i, 0), Batch(i + 2, 0), Batch(i + 3, 1))
            slots(Batch(B - 2, 0), Batch(B - 3, 1), Batch(B - 1, 1), None)
            slots(Batch(B - 1, 1), Batch(B - 2, 0), None, None)
            slots(None, Batch(B - 1, 1), None, None)

        @block.sync
        def _(sp):
            loads = [
                (in_raw, in_proj_w.rearrange("(j p) d -> p j d", p=P)),
                (conv_raw, conv_w.rearrange("(q p) o k -> p q (o k)", p=P)),
                (vec_raw[ROW_RB1:ROW_SB1, :], rb1.rearrange("e (q p) -> (e q) p", p=P)),
                (vec_raw[ROW_SB1:ROW_CONVB, :], sb1.rearrange("(q p) -> q p", p=P)),
                (vec_raw[ROW_CONVB:ROW_DTB, :], conv_b.rearrange("(q p) -> q p", p=P)),
                (vec_raw[ROW_DTB:ROW_D, :], dt_b.rearrange("(q p) -> q p", p=P)),
                (vec_raw[ROW_D:ROWS, :], d_skip.rearrange("(q p) -> q p", p=P)),
                (cond_raw, cond),
                (xp_raw[0:2 * NS, :], x_proj_w[R:R + 2 * NS, :]),
                (xp_raw[2 * NS:2 * NS + R, :], x_proj_w[0:R, :]),
                (a_raw, a_log.rearrange("(q p) n -> p q n", p=P)),
                (wmod_sb, wmod),
                (out_raw, out_proj_w),
                (router_sb[:, :], router_w),
                (router_bias[:, :], router_b.partition_broadcast(P)),
                (up_w[:, 0:E, :], rw1.rearrange("e d h -> d e h")),
                (up_w[:, E, :], sw1),
                (down_w[:, 0:E, :, :], rw2.rearrange("e (q p) d -> p e q d", p=P)),
                (down_w[:, E, :, :], sw2.rearrange("(q p) d -> p q d", p=P)),
                (down_bias[0:E, :], rb2),
                (down_bias[E:E + 1, :], sb2.rearrange("(a d) -> a d", a=1)),
            ]
            sp.dma_start(x_sb[:, :, :], x[0].rearrange("(t p) d -> p t d", p=P)).then_inc(x_in, 16)
            for dst, src in loads:
                sp.dma_start(dst, src).then_inc(w_in, 16)
            sp.wait_ge(const_made, CONSTS)
            sp.dma_start(dt_raw[:, :, 2 * NS:2 * NS + R],
                         dt_w.rearrange("(q p) r -> p q r", p=P)).then_inc(w_in, 16)
            sp.wait_ge(gate_steps, 4)
            sp.dma_start(gate_dram, gate_raw).then_inc(gates_stored, 16)
            sp.wait_ge(gates_stored, 16)

            def load_bc(b, pair):
                if not (isinstance(b.i, int) and b.i * NC + pair < BC_RING):
                    sp.wait_ge(read_done, b.i * CH + Q * (pair - BC_RING + 1))
                for which in range(2):
                    src = bc_dram[b.i, which * NS + pair * NG:which * NS + (pair + 1) * NG, :]
                    sp.dma_start(bc[:, pair % BC_RING, which, :, :].rearrange("p n t -> p (n t)"),
                                 src.rearrange("n t -> (n t)").partition_broadcast(P)
                                 ).then_inc(bc_in[pair % BC_RING], 16)

            def slots(b, a, n, m):
                if m and not (isinstance(m.i, int) and m.i == 0):
                    sp.wait_ge(xT_done, m.i)
                    sp.dma_start(x_sb[:, :, :],
                                 x[m.i].rearrange("(t p) d -> p t d", p=P)).then_inc(x_in, 16)
                if b:
                    load_bc(b, 2)
                if n:
                    sp.wait_ge(bcdt_done, n.i + 1)
                    sp.dma_start(bc_dram[n.i], bcdt[0:2 * NS, :]).then_inc(bc_stored, 16)
                if b:
                    load_bc(b, 3)
                if n:
                    sp.wait_ge(bc_stored, n.i * 16 + 16)
                    load_bc(n, 0)
                if a:
                    sp.wait_ge(out_done, a.i + 1)
                    sp.dma_start(out[a.i].rearrange("(t p) d -> p t d", p=P),
                                 out_sb[:, :, :]).then_inc(out_stored, 16)
                if b:
                    sp.dma_start(x1[:, :, :],
                                 x[b.i].rearrange("(t p) d -> p t d", p=P)).then_inc(x1_in, 16)
                    sp.dma_start(gates[:, :, :].rearrange("p g d -> p (g d)"),
                                 gate_dram[b.i].partition_broadcast(P)).then_inc(x1_in, 16)
                if n:
                    load_bc(n, 1)

            pipeline(sp, slots)
            sp.wait_ge(out_stored, 16 * B)

        @block.gpsimd
        def _(pool):
            pool.memset(ident[:, :], 0.0).then_inc(const_made, 1)
            pool.memset(before[:, :, :], 1.0).then_inc(const_made, 1)
            pool.memset(minus_half, -0.5).then_inc(const_made, 1)
            pool.memset(eps_tile, EPS).then_inc(const_made, 1)
            pool.memset(dt_raw, 0.0).then_inc(const_made, 1)
            pool.memset(w9[:, :, :], 1.0).then_inc(const_made, 1)
            pool.wait_ge(const_made, 6)
            pool.affine_select(out=ident[:, :], in_=ident[:, :], pattern=[[-1, P]],
                               compare_op=ALU.not_equal, fill=1.0, base=0,
                               channel_multiplier=1).then_inc(const_made, 1)
            pool.affine_select(out=before[:, :, :], in_=before[:, :, :], pattern=[[1, E], [-1, E]],
                               compare_op=ALU.is_gt, fill=0.0, base=0,
                               channel_multiplier=0).then_inc(const_made, 1)

            def make_rstd(which, stats, eps_added, done, b):
                pool.wait_ge(stats, b.i + 1)
                pool.tensor_tensor(rstd[:, which, :], mean_var[:, which, :, 1], eps_tile,
                                   ALU.add).then_inc(eps_added, 1)
                pool.wait_ge(eps_added, b.i + 1)
                pool.tensor_tensor(rstd[:, which, :], rstd[:, which, :], minus_half,
                                   ALU.pow).then_inc(done, 1)

            def scan_input(b, c):
                if c in POOL_INPUT_CHUNKS:
                    pair, q = c // Q, c % Q
                    if c == POOL_INPUT_CHUNKS[0]:
                        pool.wait_ge(du_done, b.i + 1)
                    pool.wait_ge(bc_in[pair % BC_RING], b.i * 64 + 32 * (pair // BC_RING + 1))
                    if not (isinstance(b.i, int) and b.i == 0 and c < STATE_RING):
                        pool.wait_ge(yacc_done, chunks_after(b, c - STATE_RING))
                    pool.tensor_tensor(state[:, c % STATE_RING, :, :], bc[:, pair % BC_RING, 0, :, :],
                                       du[:, b.p, q:q + 1, :].broadcast_to([P, NG, L]),
                                       ALU.mult).then_inc(input_pool, 1)

            def readout(b, c):
                pair = c // Q
                pool.wait_ge(scan_done, chunks_after(b, c))
                pool.tensor_tensor(state[:, c % STATE_RING, :, :], state[:, c % STATE_RING, :, :],
                                   bc[:, pair % BC_RING, 1, :, :], ALU.mult).then_inc(read_done, 1)

            def delta_x(n):
                pool.wait_ge(delta_done, Q * n.i + Q)
                pool.wait_ge(xproj_done, n.i + 1)
                pool.wait_ge(skip_done, Q * n.i + Q)
                pool.tensor_tensor(du[:, n.p, :, :], du[:, n.p, :, :], delta[:, n.p, :, :],
                                   ALU.mult).then_inc(du_done, 1)

            pool.wait_ge(setup_done, 1)

            def slots(b, a, n, m):
                for c in range(CH):
                    if b:
                        if c == 0:
                            scan_input(b, 0)
                        if c + 1 < CH:
                            scan_input(b, c + 1)
                        readout(b, c)
                    if a and c == 2:
                        make_rstd(1, stats2_done, rstd2_eps, rstd2_done, a)
                    if m and c == 3:
                        make_rstd(0, stats_done, rstd_eps, rstd_done, m)
                    if n and c == 4:
                        delta_x(n)

            pipeline(pool, slots)


        @block.tensor
        def _(pe):
            pe.wait_ge(const_made, CONSTS)
            pe.wait_ge(w_in, SET_LOADS)
            pe.wait_ge(raw_ready, 1)
            for q in range(Q):
                for k in range(KC):
                    nc.tensor.transpose(psum[:, q, k * P:(k + 1) * P], conv_in_raw[:, q, k, :],
                                        ident[:, :])
            for q in range(Q):
                nc.tensor.transpose(psum[:, 2, q * P:(q + 1) * P], in_raw[:, Q + q, :], ident[:, :])
                nc.tensor.transpose(psum[:, 3, q * 64:q * 64 + 2 * NS + R],
                                    xp_raw[:, q * P:(q + 1) * P], ident[0:2 * NS + R, 0:2 * NS + R])
                nc.tensor.transpose(psum[:, 4, q * P:(q + 1) * P], out_raw[:, q * P:(q + 1) * P],
                                    ident[:, :])
                nc.tensor.transpose(psum[0:2 * NS + R, 5, q * P:(q + 1) * P], dt_raw[:, q, :],
                                    ident[:, :])
            nc.tensor.transpose(psum[:, 6, 0:ROWS], vec_raw, ident[0:ROWS, 0:ROWS])
            nc.tensor.transpose(psum[:, 7, 448:448 + B], cond_raw,
                                ident[0:B, 0:B]).then_inc(set_mm, 1)
            pe.wait_ge(cond_silu, 1)
            for j, chunk in enumerate((SA, CA, SB, CB)):
                nc.tensor.matmul(psum[:, 7, j * B:(j + 1) * B], wmod_sb[:, chunk * DM:(chunk + 1) * DM],
                                 condT, start=True, stop=True)
            for j, chunk in enumerate((GA, GB)):
                last = nc.tensor.matmul(psum[0:B, 7, 128 + j * DM:128 + (j + 1) * DM], condT,
                                        wmod_sb[:, chunk * DM:(chunk + 1) * DM], start=True, stop=True)
            last.then_inc(set_mm, 1)
            pe.wait_ge(setup_done, 1)

            def y_start(b):
                if not (isinstance(b.i, int) and b.i == 0):
                    pe.wait_ge(gT_done, b.i)
                pe.wait_ge(skip_done, Q * b.i + Q)
                for q in range(Q):
                    for t in range(NT):
                        last = nc.tensor.matmul(Y[q][:, t * P:(t + 1) * P],
                                                skip[:, q, t * P:(t + 1) * P], ident[:, :],
                                                start=(t == 0), stop=False, is_transpose=True,
                                                skip_group_check=True)
                last.then_inc(skip_acc, 1)

            def y_add(b, c):
                q = c % Q
                pe.wait_ge(read_done, chunks_after(b, c))
                for s in range(NG):
                    for t in range(NT):
                        last = nc.tensor.matmul(Y[q][:, t * P:(t + 1) * P],
                                                state[:, c % STATE_RING, s, t * P:(t + 1) * P],
                                                ident[:, :], start=False,
                                                stop=(c >= CH - Q and s == NG - 1),
                                                is_transpose=True, skip_group_check=True)
                last.then_inc(yacc_done, 1)

            def x_transpose(m, n, a):
                pe.wait_ge(xhat_done, m.i + 1)
                if a:
                    pe.wait_ge(w9T_done, a.i + 1)
                elif n:
                    pe.wait_ge(bcdt_done, n.i + 1)
                for t in range(NT):
                    last = nc.tensor.transpose(MISC[:, t * P:(t + 1) * P], x_sb[:, t, :], ident[:, :])
                last.then_inc(xT_done, 1)

            def conv_in(n, q):
                if q == 0:
                    pe.wait_ge(h_done, n.i + 1)
                    if not (isinstance(n.i, int) and n.i < 3):
                        pe.wait_ge(gelu_done, M_UP * (n.i - 2))
                    elif n.i > 0:
                        pe.wait_ge(xb_done, Q * n.i)
                for k in range(KC):
                    last = nc.tensor.matmul(WORK[q], conv_in_wT[:, q, k, :], h_sb[:, k:k + L],
                                            start=(k == 0), stop=(k == KC - 1))
                last.then_inc(conv_done, 1)

            def z_proj(n, a):
                if a and not (isinstance(a.i, int) and a.i == 0):
                    pe.wait_ge(mixmul_done, 2 * NT * a.i)
                elif n.i > 0:
                    pe.wait_ge(delta_done, Q * n.i)
                for t in range(NT):
                    last = nc.tensor.matmul(WIDE[:, t * DI:(t + 1) * DI],
                                            h_sb[:, KC - 1 + t * P:KC - 1 + (t + 1) * P],
                                            z_wT[:, :], start=True, stop=True)
                last.then_inc(z_done, 1)

            def x_proj(n, a):
                pe.wait_ge(xb_done, Q * n.i + Q)
                if a:
                    pe.wait_ge(g_done, a.i + 1)
                for q in range(Q):
                    last = nc.tensor.matmul(MISC[0:2 * NS + R, :], xp_wT[:, q, :], du[:, n.p, q, :],
                                            start=(q == 0), stop=(q == Q - 1))
                last.then_inc(xproj_done, 1)

            def dt_proj(n):
                pe.wait_ge(bcdt_done, n.i + 1)
                pe.wait_ge(zs_done, 2 * n.i + 2)
                for q in range(Q):
                    nc.tensor.matmul(WIDE[:, q * L:(q + 1) * L], dt_wT[2 * NS:2 * NS + R, q, :],
                                     bcdt[2 * NS:2 * NS + R, :], start=True,
                                     stop=True).then_inc(dt_done, 1)

            def g_transpose(a, n):
                pe.wait_ge(gT_done, a.i + 1)
                if not (isinstance(a.i, int) and a.i == 0):
                    pe.wait_ge(fin_step, 2 * a.i)
                if n:
                    pe.wait_ge(h_done, n.i + 1)
                else:
                    pe.wait_ge(w9T_done, a.i)
                for q in range(Q):
                    for t in range(NT):
                        last = nc.tensor.transpose(G_ROWS[:, q * L + t * P:q * L + (t + 1) * P],
                                                   gT[:, t, q * P:(q + 1) * P], ident[:, :])
                last.then_inc(g_tr, 1)

            def out_proj(a):
                pe.wait_ge(g_done, a.i + 1)
                for t in range(NT):
                    for q in range(Q):
                        last = nc.tensor.matmul(OUTP[:, t * DM:(t + 1) * DM],
                                                g_soft[:, q, t * P:(t + 1) * P], out_wT[:, q, :],
                                                start=(q == 0), stop=(q == Q - 1))
                last.then_inc(oproj_done, 1)

            def x1_transpose(a, n):
                pe.wait_ge(xhat2_done, a.i + 1)
                if n:
                    pe.wait_ge(bcdt_done, n.i + 1)
                for t in range(NT):
                    last = nc.tensor.transpose(MISC[:, t * P:(t + 1) * P], xhat2[:, t, :], ident[:, :])
                last.then_inc(x1T_done, 1)

            def router(a):
                pe.wait_ge(h2_done, a.i + 1)
                for t in range(NT):
                    last = nc.tensor.matmul(MISC[:, t * E:(t + 1) * E], h2[:, t * P:(t + 1) * P],
                                            router_sb[:, :], start=True, stop=True)
                last.then_inc(router_mm, 1)

            def up(a, n, m):
                if m == 0:
                    pe.wait_ge(h2_done, a.i + 1)
                if m >= 2:
                    pe.wait_ge(gelu_done, M_UP * a.i + m - 1)
                elif n:
                    pe.wait_ge(xb_done, Q * n.i + m + 1)
                elif not (isinstance(a.i, int) and a.i == 0):
                    pe.wait_ge(gelu_done, M_UP * a.i)
                nc.tensor.matmul(WORK[m % 2], up_w[:, m // HQ, (m % HQ) * P:(m % HQ + 1) * P],
                                 h2[:, :], start=True, stop=True).then_inc(up_done, 1)

            def weights_transpose(a):
                pe.wait_ge(w9_done, a.i + 1)
                pe.wait_ge(lg_step, 3 * a.i + 1)
                for t in range(NT):
                    last = nc.tensor.transpose(MISC[0:E + 1, t * P:(t + 1) * P], w9[:, t, :],
                                               ident[:, :])
                last.then_inc(w9T_mm, 1)

            def down(a, n, t):
                ts = slice(t * P, (t + 1) * P)
                if t == 0:
                    pe.wait_ge(gelu_done, M_UP * a.i + M_UP)
                    pe.wait_ge(w9T_done, a.i + 1)
                    pe.wait_ge(gated_done, a.i + 1)
                    if n:
                        pe.wait_ge(delta_done, Q * n.i + Q)
                for q in range(HQ):
                    nc.tensor.matmul(OUTP[:, ts], h1[:, E * HQ + q, ts], down_w[:, E, q, :],
                                     start=(q == 0), stop=False)
                nc.tensor.matmul(OUTP[:, ts], w9T[:, ts], down_bias[:, :], start=False, stop=True)
                for half in range(2):
                    if t > 0:
                        pe.wait_ge(mixmul_done, 2 * NT * a.i + 2 * t - 1 + half)
                    elif not n:
                        pe.wait_ge(mixmul_done, 2 * NT * a.i)
                    for e in range(half * E // 2, (half + 1) * E // 2):
                        for q in range(HQ):
                            last = nc.tensor.matmul(WIDE[:, e * DM:(e + 1) * DM],
                                                    h1[:, e * HQ + q, ts], down_w[:, e, q, :],
                                                    start=(q == 0), stop=(q == HQ - 1))
                    last.then_inc(down_done, 1)

            def slots(b, a, n, m):
                if n:
                    conv_in(n, 0)
                if a:
                    y_add(a, CH - 1)
                if n:
                    conv_in(n, 1)
                    z_proj(n, a)
                if b:
                    y_start(b)
                if a:
                    g_transpose(a, n)
                if b:
                    y_add(b, 0)
                if n:
                    x_proj(n, a)
                if a:
                    out_proj(a)
                if n:
                    dt_proj(n)
                if b:
                    y_add(b, 1)
                if a:
                    x1_transpose(a, n)
                if a:
                    router(a)
                for k in range(M_UP):
                    if a:
                        up(a, n, k)
                    if a and k == 10:
                        weights_transpose(a)
                    if b and k == 1:
                        y_add(b, 2)
                    if b and k == 8:
                        y_add(b, 3)
                    if b and k == 14:
                        y_add(b, 4)
                for t in range(NT):
                    if a:
                        down(a, n, t)
                    if b and t == 0:
                        y_add(b, 5)
                    if m and t == 1:
                        x_transpose(m, n, a)
                    if b and t == 2:
                        y_add(b, 6)

            pipeline(pe, slots)

        @block.scalar
        def _(act):
            act.wait_ge(w_in, SET_LOADS)
            nc.scalar.activation(a_neg[:, :, :], a_raw, ACT.Exp).then_inc(a_exp, 1)
            act.wait_ge(set_mm, 1)
            nc.scalar.activation(condT, psum[:, 7, 448:448 + B], ACT.Silu).then_inc(cond_silu, 1)
            act.wait_ge(setup_done, 1)

            def decays(b, c):
                pair, q = c // Q, c % Q
                r = c % DECAY_RING
                if c == 0:
                    act.wait_ge(delta_done, Q * b.i + Q)
                if not (isinstance(b.i, int) and b.i == 0 and c < DECAY_RING):
                    act.wait_ge(scan_done, chunks_after(b, c - DECAY_RING))
                for s in range(NG):
                    k = pair * NG + s
                    last = nc.scalar.activation(decay[:, r, s, 1:L], delta[:, b.p, q, 1:L], ACT.Exp,
                                                scale=a_neg[:, q, k:k + 1])
                last.then_inc(decay_done, 1)

            def h_rows(n):
                act.wait_ge(xT_done, n.i + 1)
                if not (isinstance(n.i, int) and n.i == 0):
                    act.wait_ge(z_done, n.i)
                nc.scalar.activation(h_sb[:, KC - 1:KC - 1 + L], MISC, ACT.Identity,
                                     scale=modT[:, 1, bass.ds(n.i, 1)],
                                     bias=modT[:, 0, bass.ds(n.i, 1)]).then_inc(h_done, 1)

            def x_silu(n):
                if not (isinstance(n.i, int) and n.i < 2):
                    act.wait_ge(scan_done, (n.i - 1) * CH)
                for q in range(Q):
                    act.wait_ge(conv_done, Q * n.i + q + 1)
                    nc.scalar.activation(du[:, n.p, q, :], WORK[q], ACT.Silu,
                                         bias=vec[:, ROW_CONVB + q:ROW_CONVB + q + 1]
                                         ).then_inc(xb_done, 1)

            def skip_term(n):
                if not (isinstance(n.i, int) and n.i == 0):
                    act.wait_ge(skip_acc, n.i)
                for q in range(Q):
                    act.wait_ge(xb_done, Q * n.i + q + 1)
                    nc.scalar.activation(skip[:, q, :], du[:, n.p, q, :], ACT.Identity,
                                         scale=vec[:, ROW_D + q:ROW_D + q + 1]).then_inc(skip_done, 1)

            def z_gate(n):
                act.wait_ge(z_done, n.i + 1)
                if not (isinstance(n.i, int) and n.i < 2):
                    act.wait_ge(gT_done, n.i - 1)
                zs = z_silu[:, n.p, :, :].rearrange("p t c -> p (t c)")
                for j in range(2):
                    nc.scalar.activation(zs[:, j * 512:(j + 1) * 512], WIDE[:, j * 512:(j + 1) * 512],
                                         ACT.Silu).then_inc(zs_done, 1)

            def bcdt_rows(n):
                act.wait_ge(xproj_done, n.i + 1)
                if not (isinstance(n.i, int) and n.i == 0):
                    act.wait_ge(bc_stored, n.i * 16)
                    act.wait_ge(dt_done, Q * n.i)
                nc.scalar.activation(bcdt[:, :], MISC[0:2 * NS + R, :], ACT.Copy).then_inc(bcdt_done, 1)

            def softplus_exp(n, a):
                if a:
                    act.wait_ge(oproj_done, a.i + 1)
                for q in range(Q):
                    bias = vec[:, ROW_DTB + q:ROW_DTB + q + 1]
                    act.wait_ge(dt_done, Q * n.i + q + 1)
                    nc.scalar.activation(g_soft[:, q, :], WIDE[:, q * L:(q + 1) * L], ACT.Abs,
                                         bias=bias).then_inc(sp_abs, 1)
                    nc.scalar.activation(delta[:, n.p, q, :], WIDE[:, q * L:(q + 1) * L], ACT.Relu,
                                         bias=bias).then_inc(sp_relu, 1)
                act.wait_ge(sp_abs, Q * n.i + Q)
                nc.scalar.activation(g_soft[:, :, :], g_soft[:, :, :], ACT.Exp,
                                     scale=-1.0).then_inc(sp_exp, 1)

            def softplus_log(n):
                act.wait_ge(sp_exp, n.i + 1)
                act.wait_ge(sp_relu, Q * n.i + Q)
                nc.scalar.activation(psum[:, 4:6, :], g_soft[:, :, :], ACT.Ln,
                                     bias=1.0).then_inc(sp_ln, 1)

            def g_rows(a, n):
                act.wait_ge(g_tr, a.i + 1)
                act.wait_ge(delta_done, Q * a.i + 2 * Q if n or isinstance(a.i, int) and a.i < B - 1
                            else Q * B)
                nc.scalar.activation(g_soft[:, :, :].rearrange("p q t -> p (q t)"), G_ROWS,
                                     ACT.Copy).then_inc(g_done, 1)

            def h2_rows(a):
                act.wait_ge(x1T_done, a.i + 1)
                if not (isinstance(a.i, int) and a.i == 0):
                    act.wait_ge(up_done, M_UP * a.i)
                nc.scalar.activation(h2[:, :], MISC, ACT.Identity, scale=modT[:, 3, bass.ds(a.i, 1)],
                                     bias=modT[:, 2, bass.ds(a.i, 1)]).then_inc(h2_done, 1)

            def router_e(a):
                act.wait_ge(lg_step, 3 * a.i + 3)
                nc.scalar.activation(ex[:, :, :], lg[:, :, :], ACT.Exp).then_inc(router_exp, 1)

            def gelu(a, m):
                act.wait_ge(up_done, M_UP * a.i + m + 1)
                if m == 0 and not (isinstance(a.i, int) and a.i == 0):
                    act.wait_ge(down_done, 2 * NT * a.i)
                bias = ROW_RB1 + m
                nc.scalar.activation(h1[:, m, :], WORK[m % 2], ACT.Gelu,
                                     bias=vec[:, bias:bias + 1]).then_inc(gelu_done, 1)

            def slots(b, a, n, m):
                if n:
                    x_silu(n)
                    z_gate(n)
                    skip_term(n)
                if a:
                    g_rows(a, n)
                if b:
                    decays(b, 4)
                if n:
                    bcdt_rows(n)
                if b:
                    decays(b, 5)
                if n:
                    softplus_exp(n, a)
                if a:
                    h2_rows(a)
                if n:
                    softplus_log(n)
                if a:
                    router_e(a)
                    for k in range(M_UP):
                        gelu(a, k)
                if b:
                    decays(b, 6)
                    decays(b, 7)
                if m:
                    h_rows(m)
                if n:
                    decays(n, 0)
                    decays(n, 1)
                    decays(n, 2)
                    decays(n, 3)

            pipeline(act, slots)

        @block.vector
        def _(dve):
            nc.vector.memset(h_sb[:, 0:KC - 1], 0.0)
            nc.vector.memset(decay[:, :, :, 0:1], 0.0)
            dve.wait_ge(w_in, SET_LOADS)
            for q in range(Q):
                for k in range(KC):
                    last = nc.vector.tensor_scalar(conv_in_raw[:, q, k, :], in_raw[:, q, :],
                                                   conv_raw[:, q, k:k + 1], None, ALU.mult)
            last.then_inc(raw_ready, 1)
            dve.wait_ge(set_mm, 1)
            for q in range(Q):
                nc.vector.tensor_copy(conv_in_wT[:, q, :, :].rearrange("p k c -> p (k c)"),
                                      psum[:, q, :])
                nc.vector.tensor_copy(xp_wT[:, q, :], psum[:, 3, q * 64:q * 64 + 2 * NS + R])
            nc.vector.tensor_copy(z_wT[:, :], psum[:, 2, 0:DI])
            nc.vector.tensor_copy(out_wT[:, :, :].rearrange("p q d -> p (q d)"), psum[:, 4, 0:DI])
            nc.vector.tensor_copy(small_w[0:2 * NS + R, :],
                                  psum[0:2 * NS + R, 5, 0:Q * P])
            nc.vector.tensor_copy(vec[:, :], psum[:, 6, 0:ROWS])
            dve.wait_ge(a_exp, 1)
            nc.vector.tensor_scalar(a_neg[:, :, :], a_neg[:, :, :], -1.0, None, ALU.mult)
            dve.wait_ge(set_mm, 2)
            for j in range(4):
                nc.vector.tensor_scalar(modT[:, j, :], psum[:, 7, j * B:(j + 1) * B],
                                        float(j % 2), None, ALU.add)
            gate_ps = psum[0:B, 7, 128:128 + 2 * DM]
            nc.vector.tensor_scalar(gate_sign, gate_ps, 0.0, 2.0, ALU.is_ge,
                                    ALU.mult).then_inc(gate_steps, 1)
            nc.vector.tensor_scalar(gate_abs, gate_ps, -1.0, GATE_MIN, ALU.mult,
                                    ALU.max).then_inc(gate_steps, 1)
            dve.wait_ge(gate_steps, 2)
            nc.vector.tensor_tensor(gate_abs, gate_abs, gate_ps, ALU.max).then_inc(gate_steps, 1)
            dve.wait_ge(gate_steps, 3)
            nc.vector.scalar_tensor_tensor(out=gate_raw, in0=gate_sign, scalar=-1.0, in1=gate_abs,
                                           op0=ALU.add, op1=ALU.mult).then_inc(gate_steps, 1)
            dve.wait_ge(gates_stored, 16)
            nc.vector.memset(rsum, 0.0).then_inc(setup_done, 1)

            def stats(n):
                dve.wait_ge(x_in, 16 * n.i + 16)
                for t in range(NT):
                    last = nc.vector.bn_stats(bn[:, t, :], x_sb[:, t, :])
                last.then_inc(bn_done, 1)
                dve.wait_ge(bn_done, n.i + 1)
                nc.vector.memset(pace, 0.0)
                for t in range(NT):
                    last = nc.vector.bn_aggr(mean_var[:, 0, t, :], bn[:, t, :])
                last.then_inc(stats_done, 1)

            def xhat(n):
                dve.wait_ge(rstd_done, n.i + 1)
                for t in range(NT):
                    last = nc.vector.tensor_scalar(x_sb[:, t, :], x_sb[:, t, :],
                                                   mean_var[:, 0, t, 0:1], rstd[:, 0, t:t + 1],
                                                   ALU.subtract, ALU.mult)
                last.then_inc(xhat_done, 1)

            def make_delta(n):
                work = psum[:, 4:6, :]
                d = delta[:, n.p, :, :]
                dve.wait_ge(sp_ln, n.i + 1)
                nc.vector.tensor_tensor(d, d, work, ALU.add).then_inc(delta_step, 1)
                dve.wait_ge(delta_step, 3 * n.i + 1)
                nc.vector.tensor_scalar(work, g_soft[:, :, :], 1.0, 1.0, ALU.add,
                                        ALU.subtract).then_inc(delta_step, 1)
                nc.vector.tensor_tensor(d, d, g_soft[:, :, :], ALU.add).then_inc(delta_step, 1)
                dve.wait_ge(delta_step, 3 * n.i + 3)
                for q in range(Q):
                    nc.vector.tensor_tensor(delta[:, n.p, q, :], delta[:, n.p, q, :], WIDE[:, q * L:(q + 1) * L],
                                            ALU.subtract).then_inc(delta_done, 1)

            def scan_input(b, c):
                if c not in POOL_INPUT_CHUNKS:
                    pair, q = c // Q, c % Q
                    if c == 0:
                        dve.wait_ge(du_done, b.i + 1)
                    dve.wait_ge(bc_in[pair % BC_RING], b.i * 64 + 32 * (pair // BC_RING + 1))
                    if not (isinstance(b.i, int) and b.i == 0 and c < STATE_RING):
                        dve.wait_ge(yacc_done, chunks_after(b, c - STATE_RING))
                    nc.vector.tensor_tensor(state[:, c % STATE_RING, :, :],
                                            bc[:, pair % BC_RING, 0, :, :],
                                            du[:, b.p, q:q + 1, :].broadcast_to([P, NG, L]),
                                            ALU.mult).then_inc(input_dve, 1)

            def scan(b, c):
                scan_input(b, c)
                dve.wait_ge(decay_done, chunks_after(b, c))
                dve.wait_ge(*inputs_after(b, c))
                s = state[:, c % STATE_RING, :, :].rearrange("p n t -> p (n t)")
                nc.vector.tensor_tensor_scan(s, decay[:, c % DECAY_RING, :, :].rearrange(
                    "p n t -> p (n t)"), s, 0.0, ALU.mult, ALU.add).then_inc(scan_done, 1)

            def gate_y(a):
                dve.wait_ge(yacc_done, chunks_after(a, CH - 1))
                dve.wait_ge(zs_done, 2 * a.i + 2)
                if not (isinstance(a.i, int) and a.i == 0):
                    dve.wait_ge(mixsum_done, NT * a.i)
                nc.vector.tensor_tensor(
                    gT.rearrange("p t (q c) -> p q t c", q=Q),
                    psum[:, 0:2, :].rearrange("p q (t c) -> p q t c", t=NT),
                    z_silu[:, a.p, :, :].rearrange("p t (q c) -> p q t c", q=Q),
                    ALU.mult).then_inc(gT_done, 1)

            def residual(a):
                dve.wait_ge(oproj_done, a.i + 1)
                dve.wait_ge(x1_in, 32 * a.i + 32)
                if not (isinstance(a.i, int) and a.i == 0):
                    dve.wait_ge(out_stored, 16 * a.i)
                nc.vector.tensor_tensor(out_sb[:, :, :], OUTP.rearrange("p (t d) -> p t d", t=NT),
                                        gates[:, 0:1, :].broadcast_to([P, NT, DM]),
                                        ALU.mult).then_inc(gated_done, 1)
                dve.wait_ge(gated_done, a.i + 1)
                nc.vector.tensor_tensor(x1[:, :, :], x1[:, :, :], out_sb[:, :, :],
                                        ALU.add).then_inc(x1_done, 1)
                dve.wait_ge(x1_done, a.i + 1)
                for t in range(NT):
                    last = nc.vector.bn_stats(bn[:, t, :], x1[:, t, :])
                last.then_inc(bn2_done, 1)
                dve.wait_ge(bn2_done, a.i + 1)
                nc.vector.memset(pace, 0.0)
                for t in range(NT):
                    last = nc.vector.bn_aggr(mean_var[:, 1, t, :], bn[:, t, :])
                last.then_inc(stats2_done, 1)

            def x1hat(a):
                dve.wait_ge(rstd2_done, a.i + 1)
                for t in range(NT):
                    last = nc.vector.tensor_scalar(xhat2[:, t, :], x1[:, t, :],
                                                   mean_var[:, 1, t, 0:1], rstd[:, 1, t:t + 1],
                                                   ALU.subtract, ALU.mult)
                last.then_inc(xhat2_done, 1)

            def logits(a):
                dve.wait_ge(router_mm, a.i + 1)
                dve.wait_ge(g_tr, a.i + 1)
                nc.vector.tensor_tensor(lg[:, :, :], MISC[:, 0:NT * E].rearrange("p (t e) -> p t e", t=NT),
                                        router_bias[:, :].unsqueeze(1).broadcast_to([P, NT, E]),
                                        ALU.add).then_inc(lg_step, 1)
                dve.wait_ge(lg_step, 3 * a.i + 1)
                nc.vector.tensor_reduce(rmax, lg[:, :, :], AX.X, ALU.max).then_inc(lg_step, 1)
                dve.wait_ge(lg_step, 3 * a.i + 2)
                nc.vector.tensor_tensor(lg[:, :, :], lg[:, :, :],
                                        rmax.unsqueeze(2).broadcast_to([P, NT, E]),
                                        ALU.subtract).then_inc(lg_step, 1)

            def top2(a):
                k = 8 * a.i
                dve.wait_ge(router_exp, a.i + 1)
                nc.vector.tensor_reduce(rsum, ex[:, :, :], AX.X, ALU.add).then_inc(prob_step, 1)
                dve.wait_ge(prob_step, k + 1)
                nc.vector.reciprocal(rmax, rsum).then_inc(prob_step, 1)
                dve.wait_ge(prob_step, k + 2)
                nc.vector.tensor_tensor(pr[:, :, :], ex[:, :, :],
                                        rmax.unsqueeze(2).broadcast_to([P, NT, E]),
                                        ALU.mult).then_inc(prob_step, 1)
                dve.wait_ge(prob_step, k + 3)
                mine = pr[:, :, :].unsqueeze(3).broadcast_to([P, NT, E, E])
                other = pr[:, :, :].unsqueeze(2).broadcast_to([P, NT, E, E])
                nc.vector.tensor_tensor(gt_eq[:, 1, :, :, :], other, mine, ALU.is_equal
                                        ).then_inc(prob_step, 1)
                nc.vector.tensor_tensor(gt_eq[:, 0, :, :, :], other, mine, ALU.is_gt
                                        ).then_inc(prob_step, 1)
                dve.wait_ge(prob_step, k + 5)
                nc.vector.tensor_tensor(
                    gt_eq[:, 1, :, :, :], gt_eq[:, 1, :, :, :],
                    before[:, :, :].unsqueeze(1).broadcast_to([P, NT, E, E]),
                    ALU.mult).then_inc(prob_step, 1)
                dve.wait_ge(prob_step, k + 6)
                nc.vector.tensor_tensor(gt_eq[:, 0, :, :, :], gt_eq[:, 0, :, :, :],
                                        gt_eq[:, 1, :, :, :], ALU.add).then_inc(prob_step, 1)
                dve.wait_ge(prob_step, k + 7)
                nc.vector.tensor_reduce(rank[:, :, :], gt_eq[:, 0, :, :, :], AX.X,
                                        ALU.add).then_inc(prob_step, 1)
                dve.wait_ge(prob_step, k + 8)
                nc.vector.scalar_tensor_tensor(out=w9[:, :, 0:E], in0=rank[:, :, :], scalar=1.5,
                                               in1=pr[:, :, :], op0=ALU.is_lt,
                                               op1=ALU.mult).then_inc(w9_done, 1)

            def weights_out(a):
                dve.wait_ge(w9T_mm, a.i + 1)
                if not (isinstance(a.i, int) and a.i == 0):
                    dve.wait_ge(down_done, 2 * NT * a.i)
                nc.vector.tensor_copy(w9T[:, :], MISC[0:E + 1, :]).then_inc(w9T_done, 1)

            def mix_block(a, t):
                half_e = E // 2
                for half in range(2):
                    dve.wait_ge(down_done, 2 * (NT * a.i + t) + half + 1)
                    if half == 0 and t > 0:
                        dve.wait_ge(mixsum_done, NT * a.i + t)
                    es = slice(half * half_e, (half + 1) * half_e)
                    nc.vector.tensor_tensor(
                        mix[:, es, :], WIDE.rearrange("p (e d) -> p e d", e=E)[:, es, :],
                        w9[:, t, es].unsqueeze(2).broadcast_to([P, half_e, DM]),
                        ALU.mult).then_inc(mixmul_done, 1)
                dve.wait_ge(mixmul_done, 2 * (NT * a.i + t) + 2)
                nc.vector.tensor_reduce(out_sb[:, t, :], mix.rearrange("p e d -> p d e"), AX.X,
                                        ALU.add).then_inc(mixsum_done, 1)

            def finish(a):
                dve.wait_ge(mixsum_done, NT * a.i + NT)
                nc.vector.tensor_tensor(out_sb[:, :, :], out_sb[:, :, :],
                                        OUTP.rearrange("p (t d) -> p t d", t=NT),
                                        ALU.add).then_inc(fin_step, 1)
                dve.wait_ge(fin_step, 2 * a.i + 1)
                nc.vector.tensor_tensor(out_sb[:, :, :], out_sb[:, :, :],
                                        gates[:, 1:2, :].broadcast_to([P, NT, DM]),
                                        ALU.mult).then_inc(fin_step, 1)
                dve.wait_ge(fin_step, 2 * a.i + 2)
                nc.vector.tensor_tensor(out_sb[:, :, :], out_sb[:, :, :], x1[:, :, :],
                                        ALU.add).then_inc(out_done, 1)

            def slots(b, a, n, m):
                if b:
                    scan(b, 0)
                if a:
                    gate_y(a)
                if b:
                    scan(b, 1)
                    scan(b, 2)
                if a:
                    residual(a)
                    x1hat(a)
                if b:
                    scan(b, 3)
                if a:
                    logits(a)
                if n:
                    make_delta(n)
                if a:
                    top2(a)
                if b:
                    scan(b, 4)
                if m:
                    stats(m)
                    xhat(m)
                if a:
                    weights_out(a)
                if b:
                    scan(b, 5)
                for t in range(NT):
                    if b and t in (0, 2):
                        scan(b, 6 + t // 2)
                    if a:
                        mix_block(a, t)
                if a:
                    finish(a)

            pipeline(dve, slots)


_INS = ["L0_attn_hidden_states", "L0_attn_in_proj_w", "L0_attn_conv_w", "L0_attn_conv_b",
        "L0_attn_x_proj_w", "L0_attn_dt_w", "L0_attn_dt_b", "L0_attn_A_log", "L0_attn_D",
        "L0_attn_out_proj_w", "L0_ffn_router_w", "L0_ffn_router_b", "L0_ffn_sw1", "L0_ffn_sb1",
        "L0_ffn_sw2", "L0_ffn_sb2", "L0_ffn_rw1", "L0_ffn_rb1", "L0_ffn_rw2", "L0_ffn_rb2",
        "L0_c", "L0_wmod"]
_OUTS = [((B, L, DM), "float32")]


def kernel(**inputs):
    import numpy as _np
    import concourse.bacc as _bacc
    from concourse import mybir as _mybir
    from concourse.bass_utils import run_bass_kernel_spmd as _run

    nc = _bacc.Bacc("TRN2", target_bir_lowering=False, num_devices=1)
    arrays, args = {}, []
    for name in _INS:
        a = _np.ascontiguousarray(inputs[name])
        arrays[f"in_{name}_dram"] = a
        args.append(nc.dram_tensor(f"in_{name}_dram", a.shape, _mybir.dt.from_np(a.dtype),
                                   kind="ExternalInput").ap())
    for i, (shape, dtype) in enumerate(_OUTS):
        dt = _mybir.dt.from_np(_np.dtype(dtype))
        args.append(nc.dram_tensor(f"out_{i}_dram", shape, dt, kind="ExternalOutput").ap())
    adaln_mamba_moe_kernel(nc, *args)
    r = _run(nc, [arrays], core_ids=[0])
    return r.results[0]["out_0_dram"]
```

```python
from contextlib import ExitStack

import concourse.bass as bass
from concourse import mybir

F32 = mybir.dt.float32
F32R = mybir.dt.float32r
ALU = mybir.AluOpType
ACT = mybir.ActivationFunctionType
AX = mybir.AxisListType

B, L, DM = 8, 512, 128
DI = 2 * DM
NS = 16
R = 8
KC = 4
E, H = 8, 256
P = 128
NT = L // P
Q = DI // P
HQ = H // P
NG = 4
NC = NS // NG
CH = NC * Q
M_UP = (E + 1) * HQ
GROUPS = 2
EG = E // GROUPS
DOWNS = GROUPS * NT
H1_ROWS = EG * HQ + 3
EPS = 1e-5
GATE_MIN = 0.25
STATE_RING = 4
DECAY_RING = 4
BC_RING = 2
POOL_INPUT_CHUNKS = (1, 4, 6)
ROW_RB1, ROW_SB1, ROW_CONVB, ROW_DTB, ROW_D, ROWS = 0, 16, 18, 20, 22, 24
SA, CA, GA, SB, CB, GB = range(6)


class Batch:

    def __init__(self, index, parity):
        self.i = index
        self.p = parity


def adaln_mamba_moe_kernel(nc, x, in_proj_w, conv_w, conv_b, x_proj_w, dt_w, dt_b, a_log, d_skip,
                           out_proj_w, router_w, router_b, sw1, sb1, sw2, sb2, rw1, rb1, rw2, rb2,
                           cond, wmod, out):
    bc_dram = nc.dram_tensor("bc_rows", [B, 2 * NS, L], F32).ap()
    gate_dram = nc.dram_tensor("gate_rows", [B, 2 * DM], F32).ap()

    with ExitStack() as ctx:
        def sb(name, shape, dtype=F32):
            return ctx.enter_context(nc.sbuf_tensor(name, shape, dtype))

        def sem(name):
            return ctx.enter_context(nc.semaphore(name))

        ident = sb("ident", [P, P])
        conv_in_wT = sb("conv_in_wT", [P, Q, KC, P])
        z_wT = sb("z_wT", [P, DI])
        xp_wT = sb("xp_wT", [P, Q, 2 * NS + R])
        small_w = sb("small_w", [P, Q * P])
        out_wT = sb("out_wT", [P, Q, DM])
        router_sb = sb("router_sb", [P, E])
        router_bias = sb("router_bias", [P, E])
        up_hi = sb("up_hi", [P, E + 1, H], F32R)
        up_lo = sb("up_lo", [P, E + 1, H], F32R)
        down_w = sb("down_w", [P, E + 1, HQ, DM])
        vec = sb("vec", [P, ROWS])
        a_neg = sb("a_neg", [P, Q, NS])
        modT = sb("modT", [P, 4, B])
        constants = sb("constants", [P, 2 * NT])
        minus_half, eps_tile = constants[:, 0:NT], constants[:, NT:2 * NT]
        before = sb("before", [P, E, E], mybir.dt.bfloat16)
        x_sb = sb("x_sb", [P, NT, DM])
        h_sb = sb("h_sb", [P, KC - 1 + L])
        du = sb("du", [P, 2, Q, L])
        skip = sb("skip", [P, Q, L])
        z_silu = sb("z_silu", [P, 2, NT, DI])
        rows = sb("rows", [P, L])
        delta = sb("delta", [P, 2, Q, L])
        decay = sb("decay", [P, DECAY_RING, NG, L])
        state = sb("state", [P, STATE_RING, NG, L])
        bc = sb("bc", [P, BC_RING, 2, NG, L])
        gT_mix = sb("gT_mix", [P, NT * DI])
        g_soft = sb("g_soft", [P, Q, L])
        x1 = sb("x1", [P, NT, DM])
        gates = sb("gates", [P, 2, DM])
        h2 = sb("h2", [P, L])
        h2_hi = sb("h2_hi", [P, L], F32R)
        h2_lo = sb("h2_lo", [P, L], F32R)
        h1 = sb("h1", [P, H1_ROWS, L])
        w9 = sb("w9", [P, NT, E + 1])
        out_sb = sb("out_sb", [P, NT, DM])
        table_scratch = sb("table_scratch", [P, 4])
        bn = sb("bn", [P, NT, 6])
        mean_var = sb("mean_var", [P, 2, NT, 2])
        rstd = sb("rstd", [P, 2, NT])
        router_stats = sb("router_stats", [P, 2 * NT + 1])
        rmax, rsum = router_stats[:, 0:NT], router_stats[:, NT:2 * NT]
        pace = router_stats[:, 2 * NT:2 * NT + 1]

        gT = gT_mix[:, :].rearrange("p (t c) -> p t c", t=NT)
        mix = gT_mix[:, :].rearrange("p (g e d) -> p g e d", g=2, e=EG)
        mix_second = h2[:, :].rearrange("p (t d) -> p t d", t=NT)
        gt_eq = gT_mix[:, 0:2 * NT * E * E].rearrange("p (g t e j) -> p g t e j", g=2, t=NT, e=E)
        lg, ex, pr, rank = (gT_mix[:, k * NT * E:(k + 1) * NT * E].rearrange("p (t e) -> p t e", t=NT)
                            for k in range(2 * E, 2 * E + 4))
        gated = gT_mix[:, 0:NT * DM].rearrange("p (t d) -> p t d", t=NT)
        xhat2 = out_sb
        bcdt = rows[0:2 * NS + R, :]
        w9T = rows[64:64 + E + 1, :]
        dt_wT = small_w[0:2 * NS + R, :].rearrange("p (q d) -> p q d", q=Q)
        down_bias = small_w[64:64 + E + 1, 0:DM]
        raw = state[:, :, :, :].rearrange("p r n t -> p (r n t)")
        in_raw = raw[:, 0:4 * DM].rearrange("p (j d) -> p j d", j=4)
        conv_raw = raw[:, 512:512 + Q * KC].rearrange("p (q k) -> p q k", q=Q)
        conv_in_raw = raw[:, 1024:2048].rearrange("p (q k d) -> p q k d", q=Q, k=KC)
        xp_raw = raw[0:2 * NS + R, 2048:2048 + DI]
        dt_raw = raw[:, 2560:2560 + Q * (2 * NS + R)].rearrange("p (q r) -> p q r", q=Q)
        out_raw = raw[:, 3072:3072 + DI]
        vec_raw = raw[0:ROWS, 3584:3584 + P]
        cond_raw = raw[0:B, 3712:3712 + DM]
        condT = raw[:, 3840:3840 + B]
        a_raw = raw[:, 3904:3904 + Q * NS].rearrange("p (q n) -> p q n", q=Q)
        gate_raw = raw[0:B, 4096:4096 + 2 * DM]
        gate_sign = raw[0:B, 4352:4352 + 2 * DM]
        gate_abs = raw[0:B, 4608:4608 + 2 * DM]
        wmod_sb = raw[:, 5120:5120 + 6 * DM]
        up_raw = raw[:, 5888:5888 + (E + 1) * H].rearrange("p (e h) -> p e h", e=E + 1)

        psum = ctx.enter_context(nc.psum_tensor("psum", [P, 8, 512], F32))
        Y = (psum[:, 0, :], psum[:, 1, :])
        WORK = (psum[:, 2, :], psum[:, 3, :])
        WIDE = psum[:, 4:6, :].rearrange("p a c -> p (a c)")
        OUTP = psum[:, 6, :]
        G_ROWS = psum[:, 6:8, :].rearrange("p a c -> p (a c)")
        MISC = psum[:, 7, :]
        MOD = psum[:, 6, 0:4 * B]
        GATES = psum[0:B, 6, 128:128 + 2 * DM]

        cond_in = sem("condition_in")
        vec_in = sem("vectors_in")
        taps_in = sem("convolution_in")
        proj_in = sem("projections_in")
        experts_in = sem("experts_in")
        x_in = sem("x_in")
        x1_in = sem("residual_and_gates_in")
        bc_stored = sem("bc_stored")
        b_in = [sem(f"b_in{i}") for i in range(BC_RING)]
        c_in = [sem(f"c_in{i}") for i in range(BC_RING)]
        gates_stored = sem("gates_stored")
        out_stored = sem("out_stored")
        const_made = sem("const_made")
        raw_ready = sem("conv_scaled")
        set_mm = sem("setup_matmul")
        set_ev = sem("setup_evacuated")
        cond_silu = sem("cond_silu")
        gate_steps = sem("gate_steps")
        a_exp = sem("a_exp")
        bn_done = sem("bn_done")
        stats_done = sem("stats_done")
        rstd_eps = sem("rstd_eps")
        rstd_done = sem("rstd_done")
        xhat_done = sem("xhat_done")
        xT_done = sem("xT_done")
        h_done = sem("h_done")
        conv_done = sem("conv_done")
        xb_done = sem("xb_done")
        z_done = sem("z_done")
        zs_done = sem("zs_done")
        xproj_done = sem("xproj_done")
        bcdt_done = sem("bcdt_done")
        dt_done = sem("dt_done")
        sp_abs = sem("softplus_abs")
        sp_relu = sem("softplus_relu")
        delta_step = sem("delta_steps")
        sp_exp = sem("softplus_exp")
        sp_ln = sem("softplus_ln")
        delta_done = sem("delta_done")
        skip_done = sem("skip_done")
        du_done = sem("du_done")
        decay_done = sem("decay_done")
        input_dve = sem("input_dve")
        input_pool = sem("input_pool")
        scan_done = sem("scan_done")
        read_done = sem("readout_done")
        yacc_done = sem("yacc_done")
        skip_acc = sem("skip_accumulated")
        gT_done = sem("gT_done")
        g_tr = sem("g_transposed")
        g_done = sem("g_done")
        oproj_done = sem("oproj_done")
        gated_done = sem("gated_done")
        x1_done = sem("x1_done")
        bn2_done = sem("bn2_done")
        stats2_done = sem("stats2_done")
        rstd2_eps = sem("rstd2_eps")
        rstd2_done = sem("rstd2_done")
        xhat2_done = sem("xhat2_done")
        x1T_done = sem("x1T_done")
        h2_done = sem("h2_done")
        h2_high = sem("h2_high")
        h2_split = sem("h2_split")
        up_high = sem("up_high")
        up_split = sem("up_split")
        router_mm = sem("router_matmul")
        lg_step = sem("router_logits_steps")
        router_exp = sem("router_exp")
        prob_step = sem("router_prob_steps")
        w9_done = sem("weights_done")
        w9T_mm = sem("weights_transposed")
        w9T_done = sem("weightsT_done")
        up_done = sem("up_done")
        gelu_done = sem("gelu_done")
        down_done = sem("down_done")
        shared_done = sem("shared_done")
        mixmul_done = sem("mixmul_done")
        mixsum_done = sem("mixsum_done")
        fin_step = sem("final_steps")
        out_done = sem("out_done")
        silu_table = sem("silu_table_loaded")
        exp_table = sem("exp_table_loaded")
        gelu_table = sem("gelu_table_loaded")

        block = ctx.enter_context(nc.Block())

        def chunks_after(b, c):
            return b.i * CH + (c + 1)

        pool_inputs = len(POOL_INPUT_CHUNKS)
        dve_inputs = CH - pool_inputs

        def inputs_after(b, c):
            if c in POOL_INPUT_CHUNKS:
                return input_pool, b.i * pool_inputs + POOL_INPUT_CHUNKS.index(c) + 1
            return input_dve, b.i * dve_inputs + len([k for k in range(c + 1)
                                                      if k not in POOL_INPUT_CHUNKS])

        CONSTS = 8
        EXPERT_LOADS = 8 * 16
        MM_COND, MM_VEC, MM_MOD, MM_TAPS, MM_PROJ = range(1, 6)
        EV_MOD, EV_TAPS, EV_PROJ = range(1, 4)

        UP_ROUND = (WIDE[:, 0:L], WIDE[:, L:2 * L], WORK[0], WORK[1])
        UP_REST = (WORK[0], WORK[1], OUTP)
        UP_WIDE = H1_ROWS - 1

        def up_bank(m):
            return UP_ROUND[m % 4] if m < UP_WIDE else UP_REST[(m - UP_WIDE) % 3]

        def up_before(m):
            return max([k for k in range(m) if up_bank(k) is up_bank(m)], default=None)

        def is_last(b):
            return isinstance(b.i, int) and b.i == B - 1

        def residual_and_gates(b):
            if is_last(b):
                return x_sb[:, :, :], h_sb[:, 0:2 * DM].rearrange("p (g d) -> p g d", g=2)
            return x1[:, :, :], gates[:, :, :]

        def pipeline(eng, slots, setup=None):
            slots(None, None, None, Batch(0, 0))
            if setup:
                setup()
            slots(None, None, Batch(0, 0), Batch(1, 1))
            slots(Batch(0, 0), None, Batch(1, 1), Batch(2, 0))
            slots(Batch(1, 1), Batch(0, 0), Batch(2, 0), Batch(3, 1))
            with eng.Fori(2, B - 3, 2) as i:
                slots(Batch(i, 0), Batch(i - 1, 1), Batch(i + 1, 1), Batch(i + 2, 0))
                slots(Batch(i + 1, 1), Batch(i, 0), Batch(i + 2, 0), Batch(i + 3, 1))
            slots(Batch(B - 2, 0), Batch(B - 3, 1), Batch(B - 1, 1), None)
            slots(Batch(B - 1, 1), Batch(B - 2, 0), None, None)
            slots(None, Batch(B - 1, 1), None, None)

        @block.sync
        def _(sp):
            first = [
                (taps_in, in_raw, in_proj_w.rearrange("(j p) d -> p j d", p=P)),
                (taps_in, conv_raw, conv_w.rearrange("(q p) o k -> p q (o k)", p=P)),
                (proj_in, xp_raw[0:2 * NS, :], x_proj_w[R:R + 2 * NS, :]),
                (proj_in, xp_raw[2 * NS:2 * NS + R, :], x_proj_w[0:R, :]),
                (proj_in, out_raw, out_proj_w),
            ]
            experts = [
                (router_sb[:, :], router_w),
                (router_bias[:, :], router_b.partition_broadcast(P)),
                (up_raw[:, 0:E, :], rw1.rearrange("e d h -> d e h")),
                (up_raw[:, E, :], sw1),
                (down_w[:, 0:E, :, :], rw2.rearrange("e (q p) d -> p e q d", p=P)),
                (down_w[:, E, :, :], sw2.rearrange("(q p) d -> p q d", p=P)),
                (down_bias[0:E, :], rb2),
                (down_bias[E:E + 1, :], sb2.rearrange("(a d) -> a d", a=1)),
            ]
            sp.dma_start(x_sb[:, :, :], x[0].rearrange("(t p) d -> p t d", p=P)).then_inc(x_in, 16)
            for arrived, dst, src in first:
                sp.dma_start(dst, src).then_inc(arrived, 16)
            sp.wait_ge(const_made, CONSTS)
            sp.dma_start(dt_raw[:, :, 2 * NS:2 * NS + R],
                         dt_w.rearrange("(q p) r -> p q r", p=P)).then_inc(proj_in, 16)
            for dst, src in experts:
                sp.dma_start(dst, src).then_inc(experts_in, 16)
            sp.wait_ge(gate_steps, 4)
            sp.dma_start(gate_dram, gate_raw).then_inc(gates_stored, 16)
            sp.wait_ge(gates_stored, 16)

            def load_bc(b, pair):
                slot = pair % BC_RING
                for which, arrived in enumerate((b_in[slot], c_in[slot])):
                    if not (isinstance(b.i, int) and b.i * NC + pair < BC_RING):
                        sp.wait_ge(read_done if which else scan_done,
                                   chunks_after(b, Q * (pair - BC_RING) + Q - 1))
                    src = bc_dram[b.i, which * NS + pair * NG:which * NS + (pair + 1) * NG, :]
                    sp.dma_start(bc[:, slot, which, :, :].rearrange("p n t -> p (n t)"),
                                 src.rearrange("n t -> (n t)").partition_broadcast(P)
                                 ).then_inc(arrived, 16)

            def load_residual(b):
                residual, gate_rows = residual_and_gates(b)
                sp.dma_start(residual, x[b.i].rearrange("(t p) d -> p t d", p=P)
                             ).then_inc(x1_in, 16)
                sp.dma_start(gate_rows.rearrange("p g d -> p (g d)"),
                             gate_dram[b.i].partition_broadcast(P)).then_inc(x1_in, 16)

            def slots(b, a, n, m):
                if m and not (isinstance(m.i, int) and m.i == 0):
                    sp.wait_ge(xT_done, m.i)
                    sp.dma_start(x_sb[:, :, :],
                                 x[m.i].rearrange("(t p) d -> p t d", p=P)).then_inc(x_in, 16)
                if b:
                    load_bc(b, 2)
                if n:
                    sp.wait_ge(bcdt_done, n.i + 1)
                    sp.dma_start(bc_dram[n.i], bcdt[0:2 * NS, :]).then_inc(bc_stored, 16)
                if b:
                    load_bc(b, 3)
                if n:
                    sp.wait_ge(bc_stored, n.i * 16 + 16)
                    load_bc(n, 0)
                    load_bc(n, 1)
                if b and is_last(b):
                    sp.wait_ge(xT_done, B)
                    sp.wait_ge(z_done, 2 * B)
                    load_residual(b)
                if a:
                    sp.wait_ge(out_done, a.i + 1)
                    sp.dma_start(out[a.i].rearrange("(t p) d -> p t d", p=P),
                                 out_sb[:, :, :]).then_inc(out_stored, 16)
                if b and not is_last(b):
                    load_residual(b)

            pipeline(sp, slots)
            sp.wait_ge(out_stored, 16 * B)

        @block.gpsimd
        def _(pool):
            pool.memset(ident[:, :], 0.0).then_inc(const_made, 1)
            pool.memset(before[:, :, :], 1.0).then_inc(const_made, 1)
            pool.memset(minus_half, -0.5).then_inc(const_made, 1)
            pool.memset(eps_tile, EPS).then_inc(const_made, 1)
            pool.memset(dt_raw, 0.0).then_inc(const_made, 1)
            pool.memset(w9[:, :, :], 1.0).then_inc(const_made, 1)
            pool.wait_ge(const_made, 6)
            pool.affine_select(out=ident[:, :], in_=ident[:, :], pattern=[[-1, P]],
                               compare_op=ALU.not_equal, fill=1.0, base=0,
                               channel_multiplier=1).then_inc(const_made, 1)
            pool.affine_select(out=before[:, :, :], in_=before[:, :, :], pattern=[[1, E], [-1, E]],
                               compare_op=ALU.is_gt, fill=0.0, base=0,
                               channel_multiplier=0).then_inc(const_made, 1)

            def make_rstd(which, stats, eps_added, done, b):
                pool.wait_ge(stats, b.i + 1)
                pool.tensor_tensor(rstd[:, which, :], mean_var[:, which, :, 1], eps_tile,
                                   ALU.add).then_inc(eps_added, 1)
                pool.wait_ge(eps_added, b.i + 1)
                pool.tensor_tensor(rstd[:, which, :], rstd[:, which, :], minus_half,
                                   ALU.pow).then_inc(done, 1)

            def scan_input(b, c):
                if c in POOL_INPUT_CHUNKS:
                    pair, q = c // Q, c % Q
                    if c == POOL_INPUT_CHUNKS[0]:
                        pool.wait_ge(du_done, b.i + 1)
                    pool.wait_ge(b_in[pair % BC_RING], b.i * 32 + 16 * (pair // BC_RING + 1))
                    if not (isinstance(b.i, int) and b.i == 0 and c < STATE_RING):
                        pool.wait_ge(yacc_done, chunks_after(b, c - STATE_RING))
                    pool.tensor_tensor(state[:, c % STATE_RING, :, :], bc[:, pair % BC_RING, 0, :, :],
                                       du[:, b.p, q:q + 1, :].broadcast_to([P, NG, L]),
                                       ALU.mult).then_inc(input_pool, 1)

            def readout(b, c):
                pair = c // Q
                pool.wait_ge(scan_done, chunks_after(b, c))
                pool.wait_ge(c_in[pair % BC_RING], b.i * 32 + 16 * (pair // BC_RING + 1))
                pool.tensor_tensor(state[:, c % STATE_RING, :, :], state[:, c % STATE_RING, :, :],
                                   bc[:, pair % BC_RING, 1, :, :], ALU.mult).then_inc(read_done, 1)

            def delta_x(n):
                pool.wait_ge(delta_done, Q * n.i + Q)
                pool.wait_ge(xproj_done, n.i + 1)
                pool.wait_ge(skip_done, Q * n.i + Q)
                pool.tensor_tensor(du[:, n.p, :, :], du[:, n.p, :, :], delta[:, n.p, :, :],
                                   ALU.mult).then_inc(du_done, 1)

            def slots(b, a, n, m):
                for c in range(CH):
                    if b:
                        if c == 0:
                            scan_input(b, 0)
                        if c + 1 < CH:
                            scan_input(b, c + 1)
                        readout(b, c)
                    if a and c == 0:
                        make_rstd(1, stats2_done, rstd2_eps, rstd2_done, a)
                    if m and c == 3:
                        make_rstd(0, stats_done, rstd_eps, rstd_done, m)
                    if n and c == 6:
                        delta_x(n)

            pipeline(pool, slots)


        @block.tensor
        def _(pe):
            pe.wait_ge(const_made, CONSTS)
            pe.wait_ge(cond_in, 32)
            nc.tensor.transpose(psum[:, 2, 0:B], cond_raw, ident[0:B, 0:B]).then_inc(set_mm, 1)
            pe.wait_ge(vec_in, 6 * 16)
            nc.tensor.transpose(psum[:, 3, 0:ROWS], vec_raw,
                                ident[0:ROWS, 0:ROWS]).then_inc(set_mm, 1)

            def setup():
                pe.wait_ge(cond_silu, 1)
                for j, chunk in enumerate((SA, CA, SB, CB)):
                    nc.tensor.matmul(MOD[:, j * B:(j + 1) * B],
                                     wmod_sb[:, chunk * DM:(chunk + 1) * DM], condT,
                                     start=True, stop=True)
                for j, chunk in enumerate((GA, GB)):
                    last = nc.tensor.matmul(GATES[:, j * DM:(j + 1) * DM], condT,
                                            wmod_sb[:, chunk * DM:(chunk + 1) * DM],
                                            start=True, stop=True)
                last.then_inc(set_mm, 1)
                pe.wait_ge(raw_ready, 1)
                for q in range(Q):
                    for k in range(KC):
                        last = nc.tensor.transpose(psum[:, 4 + q, k * P:(k + 1) * P],
                                                   conv_in_raw[:, q, k, :], ident[:, :])
                last.then_inc(set_mm, 1)
                pe.wait_ge(proj_in, 4 * 16)
                for q in range(Q):
                    cols = slice(q * P, (q + 1) * P)
                    nc.tensor.transpose(psum[:, 0, cols], in_raw[:, Q + q, :], ident[:, :])
                    nc.tensor.transpose(psum[:, 0, DI + q * P:DI + (q + 1) * P], out_raw[:, cols],
                                        ident[:, :])
                    nc.tensor.transpose(psum[0:2 * NS + R, 1, cols], dt_raw[:, q, :], ident[:, :])
                    last = nc.tensor.transpose(psum[:, 1, DI + q * 64:DI + q * 64 + 2 * NS + R],
                                               xp_raw[:, cols], ident[0:2 * NS + R, 0:2 * NS + R])
                last.then_inc(set_mm, 1)

            def y_start(b):
                if not (isinstance(b.i, int) and b.i == 0):
                    pe.wait_ge(gT_done, b.i)
                pe.wait_ge(skip_done, Q * b.i + Q)
                for q in range(Q):
                    for t in range(NT):
                        last = nc.tensor.matmul(Y[q][:, t * P:(t + 1) * P],
                                                skip[:, q, t * P:(t + 1) * P], ident[:, :],
                                                start=(t == 0), stop=False, is_transpose=True,
                                                skip_group_check=True)
                last.then_inc(skip_acc, 1)

            def y_add(b, c):
                q = c % Q
                pe.wait_ge(read_done, chunks_after(b, c))
                for s in range(NG):
                    for t in range(NT):
                        last = nc.tensor.matmul(Y[q][:, t * P:(t + 1) * P],
                                                state[:, c % STATE_RING, s, t * P:(t + 1) * P],
                                                ident[:, :], start=False,
                                                stop=(c >= CH - Q and s == NG - 1),
                                                is_transpose=True, skip_group_check=True)
                last.then_inc(yacc_done, 1)

            def x_transpose(m, n, a):
                pe.wait_ge(xhat_done, m.i + 1)
                if a:
                    pe.wait_ge(w9T_done, a.i + 1)
                elif n:
                    pe.wait_ge(bcdt_done, n.i + 1)
                for t in range(NT):
                    last = nc.tensor.transpose(MISC[:, t * P:(t + 1) * P], x_sb[:, t, :], ident[:, :])
                last.then_inc(xT_done, 1)

            def conv_in(n, q, taps=range(KC)):
                if q == 0:
                    if isinstance(n.i, int) and n.i == 0:
                        pe.wait_ge(set_ev, EV_TAPS)
                    pe.wait_ge(h_done, n.i + 1)
                    if not (isinstance(n.i, int) and n.i < 3):
                        pe.wait_ge(gelu_done, M_UP * (n.i - 2))
                    elif n.i > 0:
                        pe.wait_ge(sp_relu, Q * n.i)
                for k in taps:
                    last = nc.tensor.matmul(WORK[q], conv_in_wT[:, q, k, :], h_sb[:, k:k + L],
                                            start=(k == 0), stop=(k == KC - 1))
                if k == KC - 1:
                    last.then_inc(conv_done, 1)

            def z_proj(n, a, blocks):
                if 0 in blocks:
                    if a and not (isinstance(a.i, int) and a.i == 0):
                        pe.wait_ge(mixmul_done, DOWNS * a.i)
                    elif not (isinstance(n.i, int) and n.i == 0):
                        pe.wait_ge(zs_done, 2 * n.i)
                for t in blocks:
                    last = nc.tensor.matmul(WIDE[:, t * DI:(t + 1) * DI],
                                            h_sb[:, KC - 1 + t * P:KC - 1 + (t + 1) * P],
                                            z_wT[:, :], start=True, stop=True)
                last.then_inc(z_done, 1)

            def x_proj(n, a):
                if isinstance(n.i, int) and n.i == 0:
                    pe.wait_ge(set_ev, EV_PROJ)
                pe.wait_ge(xb_done, Q * n.i + Q)
                if a:
                    pe.wait_ge(g_done, a.i + 1)
                for q in range(Q):
                    last = nc.tensor.matmul(MISC[0:2 * NS + R, :], xp_wT[:, q, :], du[:, n.p, q, :],
                                            start=(q == 0), stop=(q == Q - 1))
                last.then_inc(xproj_done, 1)

            def dt_proj(n):
                pe.wait_ge(bcdt_done, n.i + 1)
                for q in range(Q):
                    nc.tensor.matmul(WORK[q], dt_wT[2 * NS:2 * NS + R, q, :],
                                     bcdt[2 * NS:2 * NS + R, :], start=True,
                                     stop=True).then_inc(dt_done, 1)

            def g_transpose(a, n):
                pe.wait_ge(gT_done, a.i + 1)
                if not (isinstance(a.i, int) and a.i == 0):
                    pe.wait_ge(fin_step, 3 * a.i - 2)
                if n:
                    pe.wait_ge(h_done, n.i + 1)
                else:
                    pe.wait_ge(w9T_done, a.i)
                for q in range(Q):
                    for t in range(NT):
                        last = nc.tensor.transpose(G_ROWS[:, q * L + t * P:q * L + (t + 1) * P],
                                                   gT[:, t, q * P:(q + 1) * P], ident[:, :])
                last.then_inc(g_tr, 1)

            def out_proj(a):
                pe.wait_ge(g_done, a.i + 1)
                for t in range(NT):
                    for q in range(Q):
                        last = nc.tensor.matmul(OUTP[:, t * DM:(t + 1) * DM],
                                                g_soft[:, q, t * P:(t + 1) * P], out_wT[:, q, :],
                                                start=(q == 0), stop=(q == Q - 1))
                last.then_inc(oproj_done, 1)

            def x1_transpose(a, n):
                pe.wait_ge(xhat2_done, a.i + 1)
                if n:
                    pe.wait_ge(bcdt_done, n.i + 1)
                for t in range(NT):
                    last = nc.tensor.transpose(MISC[:, t * P:(t + 1) * P], xhat2[:, t, :], ident[:, :])
                last.then_inc(x1T_done, 1)

            def router(a):
                if isinstance(a.i, int) and a.i == 0:
                    pe.wait_ge(experts_in, EXPERT_LOADS)
                pe.wait_ge(h2_done, a.i + 1)
                for t in range(NT):
                    last = nc.tensor.matmul(MISC[:, t * E:(t + 1) * E], h2[:, t * P:(t + 1) * P],
                                            router_sb[:, :], start=True, stop=True)
                last.then_inc(router_mm, 1)

            def up(a, n, m):
                if m == 0:
                    if isinstance(a.i, int) and a.i == 0:
                        pe.wait_ge(up_split, 1)
                    pe.wait_ge(h2_split, a.i + 1)
                    if n:
                        pe.wait_ge(zs_done, 2 * n.i + 2)
                    else:
                        pe.wait_ge(mixmul_done, DOWNS * a.i)
                before = up_before(m)
                if before is not None:
                    pe.wait_ge(gelu_done, M_UP * a.i + before + 1)
                elif up_bank(m) is OUTP:
                    pe.wait_ge(gated_done, a.i + 1)
                elif m >= 2:
                    if n:
                        pe.wait_ge(sp_relu, Q * n.i + m - 1)
                    else:
                        pe.wait_ge(gelu_done, M_UP * a.i)
                cols = slice((m % HQ) * P, (m % HQ + 1) * P)
                high, low = up_hi[:, m // HQ, cols], up_lo[:, m // HQ, cols]
                nc.tensor.matmul(up_bank(m), high, h2_hi[:, :], start=True, stop=False)
                nc.tensor.matmul(up_bank(m), high, h2_lo[:, :], start=False, stop=False)
                nc.tensor.matmul(up_bank(m), low, h2_hi[:, :], start=False,
                                 stop=True).then_inc(up_done, 1)

            def weights_transpose(a):
                pe.wait_ge(w9_done, a.i + 1)
                pe.wait_ge(lg_step, 3 * a.i + 1)
                for t in range(NT):
                    last = nc.tensor.transpose(MISC[0:E + 1, t * P:(t + 1) * P], w9[:, t, :],
                                               ident[:, :])
                last.then_inc(w9T_mm, 1)

            def down(a, group, t):
                ts = slice(t * P, (t + 1) * P)
                if group == 0 and t < 2:
                    pe.wait_ge(gelu_done, M_UP * a.i + UP_WIDE - 1 + t)
                else:
                    pe.wait_ge(mixmul_done, DOWNS * a.i + group * NT + t - 1)
                if group > 0 and t == 0:
                    pe.wait_ge(gelu_done, M_UP * a.i + M_UP - HQ)
                wide = UP_ROUND[t % 2]
                for e in range(EG):
                    for q in range(HQ):
                        m = (group * EG + e) * HQ + q
                        last = nc.tensor.matmul(wide[:, e * DM:(e + 1) * DM], h1[:, m % H1_ROWS, ts],
                                                down_w[:, group * EG + e, q, :],
                                                start=(q == 0), stop=(q == HQ - 1))
                last.then_inc(down_done, 1)

            def shared_down(a, t):
                ts = slice(t * P, (t + 1) * P)
                if t == 0:
                    pe.wait_ge(gelu_done, M_UP * a.i + M_UP)
                    pe.wait_ge(w9T_done, a.i + 1)
                for q in range(HQ):
                    nc.tensor.matmul(OUTP[:, ts], h1[:, (E * HQ + q) % H1_ROWS, ts],
                                     down_w[:, E, q, :], start=(q == 0), stop=False)
                nc.tensor.matmul(OUTP[:, ts], w9T[:, ts], down_bias[:, :], start=False,
                                 stop=True).then_inc(shared_done, 1)

            def slots(b, a, n, m):
                if a:
                    y_add(a, CH - 1)
                if n:
                    conv_in(n, 0)
                if a:
                    g_transpose(a, n)
                if b:
                    y_start(b)
                if n:
                    conv_in(n, 1, range(1))
                if a:
                    out_proj(a)
                if n:
                    conv_in(n, 1, range(1, KC))
                if b and n:
                    y_add(b, 0)
                if n:
                    x_proj(n, a)
                    z_proj(n, a, range(NT // 2))
                if a:
                    x1_transpose(a, n)
                if b and not n:
                    y_add(b, 0)
                if n:
                    z_proj(n, a, range(NT // 2, NT))
                    dt_proj(n)
                for k in range(H1_ROWS):
                    if a:
                        up(a, n, k)
                    if a and k == 1:
                        router(a)
                    if b and k in (3, 8):
                        y_add(b, 1 + k // 8)
                for t in range(NT):
                    if a:
                        down(a, 0, t)
                    if b and t in (1, 3):
                        y_add(b, 3 + t // 2)
                    if a and t == 1:
                        weights_transpose(a)
                for k in range(H1_ROWS, M_UP):
                    if a:
                        up(a, n, k)
                if b:
                    y_add(b, 5)
                for t in range(NT):
                    if a:
                        down(a, 1, t)
                        shared_down(a, t)
                    if m and t == 1:
                        x_transpose(m, n, a)
                    if b and t == 2:
                        y_add(b, 6)

            pipeline(pe, slots, setup)

        @block.scalar
        def _(act):
            loads = [
                (cond_in, cond_raw, cond),
                (cond_in, wmod_sb, wmod),
                (vec_in, vec_raw[ROW_RB1:ROW_SB1, :], rb1.rearrange("e (q p) -> (e q) p", p=P)),
                (vec_in, vec_raw[ROW_SB1:ROW_CONVB, :], sb1.rearrange("(q p) -> q p", p=P)),
                (vec_in, vec_raw[ROW_CONVB:ROW_DTB, :], conv_b.rearrange("(q p) -> q p", p=P)),
                (vec_in, vec_raw[ROW_DTB:ROW_D, :], dt_b.rearrange("(q p) -> q p", p=P)),
                (vec_in, vec_raw[ROW_D:ROWS, :], d_skip.rearrange("(q p) -> q p", p=P)),
                (vec_in, a_raw, a_log.rearrange("(q p) n -> p q n", p=P)),
            ]
            for arrived, dst, src in loads:
                act.dma_start(dst, src).then_inc(arrived, 16)
            act.wait_ge(set_mm, MM_COND)
            nc.scalar.activation(condT, psum[:, 2, 0:B], ACT.Silu).then_inc(cond_silu, 1)

            def setup():
                act.wait_ge(vec_in, 6 * 16)
                nc.scalar.activation(a_neg[:, :, :], a_raw, ACT.Exp).then_inc(a_exp, 1)

            def load_silu_table(before):
                if not (isinstance(before, int) and before == 0):
                    act.wait_ge(silu_table, before)
                nc.scalar.activation(table_scratch[:, 0:1], eps_tile[:, 0:1],
                                     ACT.Silu).then_inc(silu_table, 1)

            def load_gelu_table(a):
                if not (isinstance(a.i, int) and a.i == 0):
                    act.wait_ge(gelu_table, a.i)
                nc.scalar.activation(table_scratch[:, 2:3], eps_tile[:, 0:1],
                                     ACT.Gelu).then_inc(gelu_table, 1)

            def load_exp_table(before):
                if not (isinstance(before, int) and before == 0):
                    act.wait_ge(exp_table, before)
                nc.scalar.activation(table_scratch[:, 1:2], eps_tile[:, 0:1],
                                     ACT.Exp).then_inc(exp_table, 1)

            def decays(b, c):
                pair, q = c // Q, c % Q
                r = c % DECAY_RING
                if c == 0:
                    act.wait_ge(delta_done, Q * b.i + Q)
                if not (isinstance(b.i, int) and b.i == 0 and c < DECAY_RING):
                    act.wait_ge(scan_done, chunks_after(b, c - DECAY_RING))
                for s in range(NG):
                    k = pair * NG + s
                    last = nc.scalar.activation(decay[:, r, s, 1:L], delta[:, b.p, q, 1:L], ACT.Exp,
                                                scale=a_neg[:, q, k:k + 1])
                last.then_inc(decay_done, 1)

            def h_rows(n):
                act.wait_ge(xT_done, n.i + 1)
                if not (isinstance(n.i, int) and n.i == 0):
                    act.wait_ge(z_done, 2 * n.i)
                else:
                    act.wait_ge(set_ev, EV_MOD)
                nc.scalar.activation(h_sb[:, KC - 1:KC - 1 + L], MISC, ACT.Identity,
                                     scale=modT[:, 1, bass.ds(n.i, 1)],
                                     bias=modT[:, 0, bass.ds(n.i, 1)]).then_inc(h_done, 1)

            def x_silu(n, q):
                if q == 0 and not (isinstance(n.i, int) and n.i < 2):
                    act.wait_ge(scan_done, (n.i - 1) * CH)
                act.wait_ge(conv_done, Q * n.i + q + 1)
                nc.scalar.activation(du[:, n.p, q, :], WORK[q], ACT.Silu,
                                     bias=vec[:, ROW_CONVB + q:ROW_CONVB + q + 1]
                                     ).then_inc(xb_done, 1)

            def skip_term(n):
                act.wait_ge(delta_done, Q * n.i + Q)
                for q in range(Q):
                    act.wait_ge(xb_done, Q * n.i + q + 1)
                    nc.scalar.activation(skip[:, q, :], du[:, n.p, q, :], ACT.Identity,
                                         scale=vec[:, ROW_D + q:ROW_D + q + 1]).then_inc(skip_done, 1)

            def z_gate(n):
                act.wait_ge(z_done, 2 * n.i + 2)
                if not (isinstance(n.i, int) and n.i < 2):
                    act.wait_ge(gT_done, n.i - 1)
                zs = z_silu[:, n.p, :, :].rearrange("p t c -> p (t c)")
                for j in range(2):
                    nc.scalar.activation(zs[:, j * 512:(j + 1) * 512], WIDE[:, j * 512:(j + 1) * 512],
                                         ACT.Silu).then_inc(zs_done, 1)

            def bcdt_rows(n):
                act.wait_ge(xproj_done, n.i + 1)
                if not (isinstance(n.i, int) and n.i == 0):
                    act.wait_ge(bc_stored, n.i * 16)
                    act.wait_ge(dt_done, Q * n.i)
                nc.scalar.activation(bcdt[:, :], MISC[0:2 * NS + R, :], ACT.Copy).then_inc(bcdt_done, 1)

            def softplus_parts(n, a):
                if a:
                    act.wait_ge(oproj_done, a.i + 1)
                if isinstance(n.i, int) and n.i == 0:
                    nc.scalar.activation(table_scratch[:, 3:4], eps_tile[:, 0:1], ACT.Exp)
                for q in range(Q):
                    bias = vec[:, ROW_DTB + q:ROW_DTB + q + 1]
                    act.wait_ge(dt_done, Q * n.i + q + 1)
                    nc.scalar.activation(g_soft[:, q, :], WORK[q], ACT.Abs,
                                         bias=bias).then_inc(sp_abs, 1)
                    nc.scalar.activation(delta[:, n.p, q, :], WORK[q], ACT.Relu,
                                         bias=bias).then_inc(sp_relu, 1)

            def softplus_log(n):
                act.wait_ge(sp_abs, Q * n.i + Q)
                nc.scalar.activation(g_soft[:, :, :], g_soft[:, :, :], ACT.Exp,
                                     scale=-1.0).then_inc(sp_exp, 1)
                act.wait_ge(sp_exp, n.i + 1)
                act.wait_ge(sp_relu, Q * n.i + Q)
                if not (isinstance(n.i, int) and n.i == 0):
                    act.wait_ge(skip_acc, n.i)
                nc.scalar.activation(skip[:, :, :], g_soft[:, :, :], ACT.Ln,
                                     bias=1.0).then_inc(sp_ln, 1)

            def g_rows(a, n):
                act.wait_ge(g_tr, a.i + 1)
                act.wait_ge(delta_done, Q * a.i + 2 * Q if n or isinstance(a.i, int) and a.i < B - 1
                            else Q * B)
                nc.scalar.activation(g_soft[:, :, :].rearrange("p q t -> p (q t)"), G_ROWS,
                                     ACT.Copy).then_inc(g_done, 1)

            def h2_rows(a):
                act.wait_ge(x1T_done, a.i + 1)
                if not (isinstance(a.i, int) and a.i == 0):
                    act.wait_ge(fin_step, 3 * a.i - 1)
                nc.scalar.activation(h2[:, :], MISC, ACT.Identity, scale=modT[:, 3, bass.ds(a.i, 1)],
                                     bias=modT[:, 2, bass.ds(a.i, 1)]).then_inc(h2_done, 1)
                nc.scalar.activation(h2_hi[:, :], MISC, ACT.Identity,
                                     scale=modT[:, 3, bass.ds(a.i, 1)],
                                     bias=modT[:, 2, bass.ds(a.i, 1)]).then_inc(h2_high, 1)

            def router_e(a):
                act.wait_ge(lg_step, 3 * a.i + 3)
                nc.scalar.activation(ex[:, :, :], lg[:, :, :], ACT.Exp).then_inc(router_exp, 1)

            def weights_out(a):
                act.wait_ge(w9T_mm, a.i + 1)
                if not (isinstance(a.i, int) and a.i == 0):
                    act.wait_ge(shared_done, NT * a.i)
                nc.scalar.activation(w9T[:, :], MISC[0:E + 1, :], ACT.Copy).then_inc(w9T_done, 1)

            def gelu(a, m):
                act.wait_ge(up_done, M_UP * a.i + m + 1)
                if m >= H1_ROWS:
                    act.wait_ge(down_done, DOWNS * a.i + NT)
                elif m == 0 and not (isinstance(a.i, int) and a.i == 0):
                    act.wait_ge(shared_done, NT * a.i)
                bias = ROW_RB1 + m
                nc.scalar.activation(h1[:, m % H1_ROWS, :], up_bank(m), ACT.Gelu,
                                     bias=vec[:, bias:bias + 1]).then_inc(gelu_done, 1)

            def slots(b, a, n, m):
                if n:
                    load_silu_table(2 * n.i)
                    x_silu(n, 0)
                if a:
                    g_rows(a, n)
                if b:
                    decays(b, 4)
                if n:
                    load_silu_table(2 * n.i + 1)
                    x_silu(n, 1)
                    bcdt_rows(n)
                if a:
                    h2_rows(a)
                if n:
                    z_gate(n)
                    softplus_parts(n, a)
                if a:
                    load_exp_table(a.i)
                    router_e(a)
                    for k in range(H1_ROWS):
                        gelu(a, k)
                if b:
                    decays(b, 5)
                    decays(b, 6)
                if a:
                    weights_out(a)
                if b and not n:
                    decays(b, 7)
                if n:
                    softplus_log(n)
                if a:
                    load_gelu_table(a)
                    for k in range(H1_ROWS, M_UP):
                        gelu(a, k)
                if b and n:
                    decays(b, 7)
                if n:
                    skip_term(n)
                    decays(n, 0)
                    decays(n, 1)
                if m:
                    h_rows(m)
                if n:
                    decays(n, 2)
                    decays(n, 3)

            pipeline(act, slots, setup)

        @block.vector
        def _(dve):
            nc.vector.memset(h_sb[:, 0:KC - 1], 0.0)
            nc.vector.memset(decay[:, :, :, 0:1], 0.0)

            def setup():
                dve.wait_ge(set_mm, MM_VEC)
                nc.vector.tensor_copy(vec[:, :], psum[:, 3, 0:ROWS])
                dve.wait_ge(taps_in, 2 * 16)
                for q in range(Q):
                    for k in range(KC):
                        last = nc.vector.tensor_scalar(conv_in_raw[:, q, k, :], in_raw[:, q, :],
                                                       conv_raw[:, q, k:k + 1], None, ALU.mult)
                last.then_inc(raw_ready, 1)
                dve.wait_ge(set_mm, MM_MOD)
                for j in range(4):
                    last = nc.vector.tensor_scalar(modT[:, j, :], MOD[:, j * B:(j + 1) * B],
                                                   float(j % 2), None, ALU.add)
                last.then_inc(set_ev, 1)
                dve.wait_ge(set_mm, MM_TAPS)
                for q in range(Q):
                    last = nc.vector.tensor_copy(
                        conv_in_wT[:, q, :, :].rearrange("p k c -> p (k c)"), psum[:, 4 + q, :])
                last.then_inc(set_ev, 1)
                dve.wait_ge(set_mm, MM_PROJ)
                nc.vector.tensor_copy(z_wT[:, :], psum[:, 0, 0:DI])
                nc.vector.tensor_copy(out_wT[:, :, :].rearrange("p q d -> p (q d)"),
                                      psum[:, 0, DI:2 * DI])
                nc.vector.tensor_copy(small_w[0:2 * NS + R, :], psum[0:2 * NS + R, 1, 0:DI])
                for q in range(Q):
                    last = nc.vector.tensor_copy(xp_wT[:, q, :],
                                                 psum[:, 1, DI + q * 64:DI + q * 64 + 2 * NS + R])
                last.then_inc(set_ev, 1)
                nc.vector.tensor_scalar(gate_sign, GATES, 0.0, 2.0, ALU.is_ge,
                                        ALU.mult).then_inc(gate_steps, 1)
                nc.vector.tensor_scalar(gate_abs, GATES, -1.0, GATE_MIN, ALU.mult,
                                        ALU.max).then_inc(gate_steps, 1)
                dve.wait_ge(gate_steps, 2)
                nc.vector.tensor_tensor(gate_abs, gate_abs, GATES, ALU.max).then_inc(gate_steps, 1)
                dve.wait_ge(gate_steps, 3)
                nc.vector.scalar_tensor_tensor(out=gate_raw, in0=gate_sign, scalar=-1.0,
                                               in1=gate_abs, op0=ALU.add,
                                               op1=ALU.mult).then_inc(gate_steps, 1)
                dve.wait_ge(a_exp, 1)
                nc.vector.tensor_scalar(a_neg[:, :, :], a_neg[:, :, :], -1.0, None, ALU.mult)
                dve.wait_ge(gates_stored, 16)

            def stats(n):
                dve.wait_ge(x_in, 16 * n.i + 16)
                for t in range(NT):
                    last = nc.vector.bn_stats(bn[:, t, :], x_sb[:, t, :])
                last.then_inc(bn_done, 1)
                dve.wait_ge(bn_done, n.i + 1)
                nc.vector.memset(pace, 0.0)
                for t in range(NT):
                    last = nc.vector.bn_aggr(mean_var[:, 0, t, :], bn[:, t, :])
                last.then_inc(stats_done, 1)

            def xhat(n):
                dve.wait_ge(rstd_done, n.i + 1)
                for t in range(NT):
                    last = nc.vector.tensor_scalar(x_sb[:, t, :], x_sb[:, t, :],
                                                   mean_var[:, 0, t, 0:1], rstd[:, 0, t:t + 1],
                                                   ALU.subtract, ALU.mult)
                last.then_inc(xhat_done, 1)

            def make_delta(n):
                e = g_soft[:, :, :]
                d = delta[:, n.p, :, :]
                dve.wait_ge(sp_relu, Q * n.i + Q)
                dve.wait_ge(sp_exp, n.i + 1)
                nc.vector.tensor_tensor(d, d, e, ALU.add).then_inc(delta_step, 1)
                dve.wait_ge(delta_step, 3 * n.i + 1)
                dve.wait_ge(sp_ln, n.i + 1)
                nc.vector.tensor_scalar(e, e, 1.0, 1.0, ALU.add,
                                        ALU.subtract).then_inc(delta_step, 1)
                dve.wait_ge(delta_step, 3 * n.i + 2)
                nc.vector.tensor_tensor(d, d, e, ALU.subtract).then_inc(delta_step, 1)
                dve.wait_ge(delta_step, 3 * n.i + 3)
                for q in range(Q):
                    nc.vector.tensor_tensor(delta[:, n.p, q, :], delta[:, n.p, q, :],
                                            skip[:, q, :], ALU.add).then_inc(delta_done, 1)

            def scan_input(b, c):
                if c not in POOL_INPUT_CHUNKS:
                    pair, q = c // Q, c % Q
                    if c == 0:
                        dve.wait_ge(du_done, b.i + 1)
                    dve.wait_ge(b_in[pair % BC_RING], b.i * 32 + 16 * (pair // BC_RING + 1))
                    if not (isinstance(b.i, int) and b.i == 0 and c < STATE_RING):
                        dve.wait_ge(yacc_done, chunks_after(b, c - STATE_RING))
                    nc.vector.tensor_tensor(state[:, c % STATE_RING, :, :],
                                            bc[:, pair % BC_RING, 0, :, :],
                                            du[:, b.p, q:q + 1, :].broadcast_to([P, NG, L]),
                                            ALU.mult).then_inc(input_dve, 1)

            def scan(b, c):
                dve.wait_ge(decay_done, chunks_after(b, c))
                dve.wait_ge(*inputs_after(b, c))
                s = state[:, c % STATE_RING, :, :].rearrange("p n t -> p (n t)")
                nc.vector.tensor_tensor_scan(s, decay[:, c % DECAY_RING, :, :].rearrange(
                    "p n t -> p (n t)"), s, 0.0, ALU.mult, ALU.add).then_inc(scan_done, 1)

            def gate_y(a):
                dve.wait_ge(yacc_done, chunks_after(a, CH - 1))
                dve.wait_ge(zs_done, 2 * a.i + 2)
                if not (isinstance(a.i, int) and a.i == 0):
                    dve.wait_ge(mixsum_done, DOWNS * a.i)
                nc.vector.tensor_tensor(
                    gT.rearrange("p t (q c) -> p q t c", q=Q),
                    psum[:, 0:2, :].rearrange("p q (t c) -> p q t c", t=NT),
                    z_silu[:, a.p, :, :].rearrange("p t (q c) -> p q t c", q=Q),
                    ALU.mult).then_inc(gT_done, 1)

            def residual(a):
                x1_tile, gate_rows = residual_and_gates(a)
                dve.wait_ge(oproj_done, a.i + 1)
                dve.wait_ge(x1_in, 32 * a.i + 32)
                nc.vector.tensor_tensor(gated, OUTP.rearrange("p (t d) -> p t d", t=NT),
                                        gate_rows[:, 0:1, :].broadcast_to([P, NT, DM]),
                                        ALU.mult).then_inc(gated_done, 1)
                dve.wait_ge(gated_done, a.i + 1)
                nc.vector.tensor_tensor(x1_tile, x1_tile, gated,
                                        ALU.add).then_inc(x1_done, 1)
                dve.wait_ge(x1_done, a.i + 1)
                for t in range(NT):
                    last = nc.vector.bn_stats(bn[:, t, :], x1_tile[:, t, :])
                last.then_inc(bn2_done, 1)
                dve.wait_ge(bn2_done, a.i + 1)
                nc.vector.memset(pace, 0.0)
                for t in range(NT):
                    last = nc.vector.bn_aggr(mean_var[:, 1, t, :], bn[:, t, :])
                last.then_inc(stats2_done, 1)

            def x1hat(a):
                x1_tile, _ = residual_and_gates(a)
                dve.wait_ge(rstd2_done, a.i + 1)
                if not (isinstance(a.i, int) and a.i == 0):
                    dve.wait_ge(out_stored, 16 * a.i)
                for t in range(NT):
                    last = nc.vector.tensor_scalar(xhat2[:, t, :], x1_tile[:, t, :],
                                                   mean_var[:, 1, t, 0:1], rstd[:, 1, t:t + 1],
                                                   ALU.subtract, ALU.mult)
                last.then_inc(xhat2_done, 1)

            def logits(a):
                if isinstance(a.i, int) and a.i == 0:
                    dve.wait_ge(experts_in, EXPERT_LOADS)
                dve.wait_ge(router_mm, a.i + 1)
                dve.wait_ge(g_tr, a.i + 1)
                nc.vector.tensor_tensor(lg[:, :, :], MISC[:, 0:NT * E].rearrange("p (t e) -> p t e", t=NT),
                                        router_bias[:, :].unsqueeze(1).broadcast_to([P, NT, E]),
                                        ALU.add).then_inc(lg_step, 1)
                dve.wait_ge(lg_step, 3 * a.i + 1)
                nc.vector.tensor_reduce(rmax, lg[:, :, :], AX.X, ALU.max).then_inc(lg_step, 1)
                dve.wait_ge(lg_step, 3 * a.i + 2)
                nc.vector.tensor_tensor(lg[:, :, :], lg[:, :, :],
                                        rmax.unsqueeze(2).broadcast_to([P, NT, E]),
                                        ALU.subtract).then_inc(lg_step, 1)

            def top2(a):
                k = 8 * a.i
                dve.wait_ge(router_exp, a.i + 1)
                nc.vector.tensor_reduce(rsum, ex[:, :, :], AX.X, ALU.add).then_inc(prob_step, 1)
                dve.wait_ge(prob_step, k + 1)
                nc.vector.reciprocal(rmax, rsum).then_inc(prob_step, 1)
                dve.wait_ge(prob_step, k + 2)
                nc.vector.tensor_tensor(pr[:, :, :], ex[:, :, :],
                                        rmax.unsqueeze(2).broadcast_to([P, NT, E]),
                                        ALU.mult).then_inc(prob_step, 1)
                dve.wait_ge(prob_step, k + 3)
                mine = pr[:, :, :].unsqueeze(3).broadcast_to([P, NT, E, E])
                other = pr[:, :, :].unsqueeze(2).broadcast_to([P, NT, E, E])
                nc.vector.tensor_tensor(gt_eq[:, 1, :, :, :], other, mine, ALU.is_equal
                                        ).then_inc(prob_step, 1)
                nc.vector.tensor_tensor(gt_eq[:, 0, :, :, :], other, mine, ALU.is_gt
                                        ).then_inc(prob_step, 1)
                dve.wait_ge(prob_step, k + 5)
                nc.vector.tensor_tensor(
                    gt_eq[:, 1, :, :, :], gt_eq[:, 1, :, :, :],
                    before[:, :, :].unsqueeze(1).broadcast_to([P, NT, E, E]),
                    ALU.mult).then_inc(prob_step, 1)
                dve.wait_ge(prob_step, k + 6)
                nc.vector.tensor_tensor(gt_eq[:, 0, :, :, :], gt_eq[:, 0, :, :, :],
                                        gt_eq[:, 1, :, :, :], ALU.add).then_inc(prob_step, 1)
                dve.wait_ge(prob_step, k + 7)
                nc.vector.tensor_reduce(rank[:, :, :], gt_eq[:, 0, :, :, :], AX.X,
                                        ALU.add).then_inc(prob_step, 1)
                dve.wait_ge(prob_step, k + 8)
                nc.vector.scalar_tensor_tensor(out=w9[:, :, 0:E], in0=rank[:, :, :], scalar=1.5,
                                               in1=pr[:, :, :], op0=ALU.is_lt,
                                               op1=ALU.mult).then_inc(w9_done, 1)

            def mix_block(a, group, t):
                j = group * NT + t
                if j == 0:
                    dve.wait_ge(w9_done, a.i + 1)
                dve.wait_ge(down_done, DOWNS * a.i + j + 1)
                if j >= 2:
                    dve.wait_ge(mixsum_done, DOWNS * a.i + j - 1)
                nc.vector.tensor_tensor(
                    mix[:, j % 2, :, :], UP_ROUND[t % 2].rearrange("p (e d) -> p e d", e=EG),
                    w9[:, t, group * EG:(group + 1) * EG].unsqueeze(2).broadcast_to([P, EG, DM]),
                    ALU.mult).then_inc(mixmul_done, 1)
                dve.wait_ge(mixmul_done, DOWNS * a.i + j + 1)
                nc.vector.tensor_reduce((mix_second if group else out_sb)[:, t, :],
                                        mix[:, j % 2, :, :].rearrange("p e d -> p d e"), AX.X,
                                        ALU.add).then_inc(mixsum_done, 1)

            def split_up_weights():
                dve.wait_ge(experts_in, EXPERT_LOADS)
                nc.vector.tensor_copy(up_hi[:, :, :], up_raw).then_inc(up_high, 1)
                dve.wait_ge(up_high, 1)
                nc.vector.tensor_tensor(up_lo[:, :, :], up_raw, up_hi[:, :, :].bitcast(F32),
                                        ALU.subtract).then_inc(up_split, 1)

            def split_h2(a):
                dve.wait_ge(h2_high, a.i + 1)
                if not (isinstance(a.i, int) and a.i == 0):
                    dve.wait_ge(up_done, M_UP * a.i)
                nc.vector.tensor_tensor(h2_lo[:, :], h2[:, :], h2_hi[:, :].bitcast(F32),
                                        ALU.subtract).then_inc(h2_split, 1)

            def finish_sum(a):
                dve.wait_ge(mixsum_done, DOWNS * a.i + DOWNS)
                dve.wait_ge(shared_done, NT * a.i + NT)
                nc.vector.tensor_tensor(out_sb[:, :, :], out_sb[:, :, :],
                                        OUTP.rearrange("p (t d) -> p t d", t=NT),
                                        ALU.add).then_inc(fin_step, 1)

            def finish(a):
                x1_tile, gate_rows = residual_and_gates(a)
                dve.wait_ge(fin_step, 3 * a.i + 1)
                nc.vector.tensor_tensor(out_sb[:, :, :], out_sb[:, :, :], mix_second,
                                        ALU.add).then_inc(fin_step, 1)
                dve.wait_ge(fin_step, 3 * a.i + 2)
                nc.vector.tensor_tensor(out_sb[:, :, :], out_sb[:, :, :],
                                        gate_rows[:, 1:2, :].broadcast_to([P, NT, DM]),
                                        ALU.mult).then_inc(fin_step, 1)
                dve.wait_ge(fin_step, 3 * a.i + 3)
                nc.vector.tensor_tensor(out_sb[:, :, :], out_sb[:, :, :], x1_tile,
                                        ALU.add).then_inc(out_done, 1)

            def slots(b, a, n, m):
                if b:
                    scan(b, 1)
                if a:
                    residual(a)
                if b:
                    scan_input(b, 2)
                if a:
                    x1hat(a)
                if b:
                    scan(b, 2)
                if a:
                    split_h2(a)
                if b:
                    scan_input(b, 3)
                if a:
                    logits(a)
                if b:
                    scan(b, 3)
                if a:
                    top2(a)
                if b:
                    scan(b, 4)
                if m:
                    stats(m)
                if b:
                    scan_input(b, 5)
                for t in range(NT):
                    if a:
                        mix_block(a, 0, t)
                    if m and t == 0:
                        xhat(m)
                    if b and t == 1:
                        scan(b, 5)
                if n and b and not a:
                    make_delta(n)
                if b:
                    scan(b, 6)
                if n and isinstance(n.i, int) and n.i == 0:
                    split_up_weights()
                if b:
                    scan_input(b, 7)
                if n and (a or not b):
                    make_delta(n)
                if a:
                    mix_block(a, 1, 0)
                if b:
                    scan(b, 7)
                if a:
                    mix_block(a, 1, 1)
                    mix_block(a, 1, 2)
                if n:
                    scan_input(n, 0)
                if a:
                    mix_block(a, 1, 3)
                    finish_sum(a)
                if a and n:
                    finish(a)
                if b:
                    gate_y(b)
                if a and not n:
                    finish(a)
                if n:
                    scan(n, 0)

            pipeline(dve, slots, setup)


_INS = ["L0_attn_hidden_states", "L0_attn_in_proj_w", "L0_attn_conv_w", "L0_attn_conv_b",
        "L0_attn_x_proj_w", "L0_attn_dt_w", "L0_attn_dt_b", "L0_attn_A_log", "L0_attn_D",
        "L0_attn_out_proj_w", "L0_ffn_router_w", "L0_ffn_router_b", "L0_ffn_sw1", "L0_ffn_sb1",
        "L0_ffn_sw2", "L0_ffn_sb2", "L0_ffn_rw1", "L0_ffn_rb1", "L0_ffn_rw2", "L0_ffn_rb2",
        "L0_c", "L0_wmod"]
_OUTS = [((B, L, DM), "float32")]


def kernel(**inputs):
    import numpy as _np
    import concourse.bacc as _bacc
    from concourse import mybir as _mybir
    from concourse.bass_utils import run_bass_kernel_spmd as _run

    nc = _bacc.Bacc("TRN2", target_bir_lowering=False, num_devices=1)
    arrays, args = {}, []
    for name in _INS:
        a = _np.ascontiguousarray(inputs[name])
        arrays[f"in_{name}_dram"] = a
        args.append(nc.dram_tensor(f"in_{name}_dram", a.shape, _mybir.dt.from_np(a.dtype),
                                   kind="ExternalInput").ap())
    for i, (shape, dtype) in enumerate(_OUTS):
        dt = _mybir.dt.from_np(_np.dtype(dtype))
        args.append(nc.dram_tensor(f"out_{i}_dram", shape, dt, kind="ExternalOutput").ap())
    adaln_mamba_moe_kernel(nc, *args)
    r = _run(nc, [arrays], core_ids=[0])
    return r.results[0]["out_0_dram"]
```
